# Optimizing a Trainium2 kernel written in Bass

```python
import numpy as np
import jax
import jax.numpy as jnp

def _softmax(x, axis=-1):
    return jax.nn.softmax(x, axis=axis)

def _gelu(x):
    return jax.nn.gelu(x, approximate=True)

def _silu(x):
    return jax.nn.silu(x)

def _sigmoid(x):
    return jax.nn.sigmoid(x)

def _layernorm(x, axis=-1, eps=1e-05):
    m = jnp.mean(x, axis=axis, keepdims=True)
    v = jnp.var(x, axis=axis, keepdims=True)
    return (x - m) / jnp.sqrt(v + eps)

def _scatter_add(tgt, idx, src, axis=0):
    return tgt.at[idx].add(src)

def _segment_sum(src, seg, n):
    return jax.ops.segment_sum(src, seg, n)
kernel_name = 'mk_adj_ffn_d1_adj_r2_506bd7'

def setup_inputs(seed: int=0):
    np.random.seed(seed)
    _w = jnp.asarray

    def _rec_inputs():
        import jax
        import jax.numpy as jnp
        _gk = jax.random.key(seed)
        x = -0.0002928 + 1 * jax.random.normal(jax.random.fold_in(_gk, 1), (128, 128, 128), jnp.float32)
        _a = jax.random.bernoulli(jax.random.fold_in(_gk, 2), 0.0625, (128, 128, 128))
        _a = jnp.logical_or(_a, jnp.swapaxes(_a, -1, -2))
        _a = jnp.logical_or(_a, jnp.eye(128, dtype=bool))
        adj = _a.astype(jnp.int32)
        return (x, adj)
    x, adj = _rec_inputs()

    def _L0_gnn_setup():
        import jax, jax.numpy as jnp
        import numpy as np
        key = jax.random.key(seed)
        k1, k2, k3, k4 = jax.random.split(key, 4)
        B, N, F, U = (8, 1024, 128, 128)
        x = jax.random.normal(k1, (B, N, F), dtype=jnp.float32)
        adj = jax.random.randint(k2, (B, N, N), 0, 2, dtype=jnp.int32)
        W_msg = jax.random.normal(k3, (F, U), dtype=jnp.float32) / np.sqrt(F)
        W_upd = jax.random.normal(k4, (F, U), dtype=jnp.float32) / np.sqrt(F)
        bias = jnp.zeros((U,), dtype=jnp.float32)
        return {'x': x, 'adj': adj, 'W_msg': W_msg, 'W_upd': W_upd, 'bias': bias}
    _L0_gnn_all = _L0_gnn_setup()
    _L0_gnn_in = {k: v for k, v in _L0_gnn_all.items() if k in ('W_msg', 'W_upd', 'bias')}
    del _L0_gnn_all

    def _L0_ffn_setup():
        import jax, jax.numpy as jnp
        import numpy as np
        B, T, D, H, E = (16, 2048, 128, 256, 8)
        key = jax.random.key(seed)
        ks = jax.random.split(key, 5)
        x = jax.random.normal(ks[0], (B, T, D), dtype=jnp.float32)
        gate_w = jax.random.normal(ks[1], (D, E), dtype=jnp.float32) * 0.02
        gate_b = jnp.zeros((E,), dtype=jnp.float32)
        W1 = jax.random.normal(ks[2], (E, D, H), dtype=jnp.float32) * 0.02
        b1 = jnp.zeros((E, H), dtype=jnp.float32)
        W2 = jax.random.normal(ks[3], (E, H, D), dtype=jnp.float32) * 0.02
        b2 = jnp.zeros((E, D), dtype=jnp.float32)
        return {'x': x, 'gate_w': gate_w, 'gate_b': gate_b, 'W1': W1, 'b1': b1, 'W2': W2, 'b2': b2}
    _L0_ffn_all = _L0_ffn_setup()
    _L0_ffn_in = {k: v for k, v in _L0_ffn_all.items() if k in ('gate_w', 'gate_b', 'W1', 'b1', 'W2', 'b2')}
    del _L0_ffn_all
    return {'x': x, 'adj': adj, 'L0_gnn_W_msg': _L0_gnn_in['W_msg'], 'L0_gnn_W_upd': _L0_gnn_in['W_upd'], 'L0_gnn_bias': _L0_gnn_in['bias'], 'L0_ffn_gate_w': _L0_ffn_in['gate_w'], 'L0_ffn_gate_b': _L0_ffn_in['gate_b'], 'L0_ffn_W1': _L0_ffn_in['W1'], 'L0_ffn_b1': _L0_ffn_in['b1'], 'L0_ffn_W2': _L0_ffn_in['W2'], 'L0_ffn_b2': _L0_ffn_in['b2']}

def reference(x, adj, L0_gnn_W_msg, L0_gnn_W_upd, L0_gnn_bias, L0_ffn_gate_w, L0_ffn_gate_b, L0_ffn_W1, L0_ffn_b1, L0_ffn_W2, L0_ffn_b2):
    import jax
    import jax.numpy as jnp

    def _L0_gnn_ref(x, adj, W_msg, W_upd, bias):
        import jax, jax.numpy as jnp
        import numpy as np
        a = adj.astype(x.dtype)
        h = jnp.einsum('bnf,fu->bnu', x, W_msg)
        msg_sum = jnp.einsum('bij,biu->bju', a, h)
        deg = jnp.sum(a, axis=1)
        messages = jnp.where(deg[..., None] > 0, msg_sum / jnp.maximum(deg, 1.0)[..., None], 0.0)
        out = jnp.einsum('bnf,fu->bnu', x, W_upd) + messages + bias
        return jax.nn.relu(out)

    def _L0_ffn_ref(x, gate_w, gate_b, W1, b1, W2, b2):
        import jax, jax.numpy as jnp
        import numpy as np
        B, T, D, H, E = (16, 2048, 128, 256, 8)
        Bb, Tt, Dd = x.shape
        Ee = gate_w.shape[1]
        xf = x.reshape(-1, Dd)
        N = xf.shape[0]
        logits = xf @ gate_w + gate_b
        probs = jax.nn.softmax(logits, axis=-1)
        top2_vals, top2_idx = jax.lax.top_k(probs, 2)
        cw = jnp.zeros((N, Ee), dtype=xf.dtype).at[jnp.arange(N)[:, None], top2_idx].add(top2_vals)

        def step(acc, params):
            w1, bb1, w2, bb2, we = params
            h = jax.nn.gelu(xf @ w1 + bb1, approximate=False)
            y = h @ w2 + bb2
            return (acc + we[:, None] * y, None)
        out, _ = jax.lax.scan(step, jnp.zeros_like(xf), (W1, b1, W2, b2, cw.T))
        return out.reshape(Bb, Tt, Dd)
    x = x + _L0_gnn_ref(_layernorm(x, axis=-1), adj, L0_gnn_W_msg, L0_gnn_W_upd, L0_gnn_bias)
    x = x + _L0_ffn_ref(_layernorm(x, axis=-1), L0_ffn_gate_w, L0_ffn_gate_b, L0_ffn_W1, L0_ffn_b1, L0_ffn_W2, L0_ffn_b2)
    return x

_drawn_inputs = setup_inputs


def setup_inputs(seed=0):
    import zlib

    import numpy as np

    out = dict(_drawn_inputs(seed))
    spreads = {'L0_gnn_bias': (0.0, 0.1),
     'L0_ffn_gate_b': (0.0, 0.593),
     'L0_ffn_b1': (0.0, 0.8),
     'L0_ffn_b2': (0.0, 0.44)}
    factors = {'L0_ffn_gate_w': 3.375, 'L0_ffn_W1': 7.88, 'L0_ffn_W2': 7.158}
    for name, (base, spread) in spreads.items():
        noise = np.random.default_rng([zlib.crc32(name.encode()), seed]).standard_normal(out[name].shape)
        drawn = base * np.exp(spread * noise) if base else spread * noise
        out[name] = jnp.asarray(drawn.astype(out[name].dtype))
    for name, factor in factors.items():
        out[name] = (out[name] * factor).astype(out[name].dtype)
    return out
```

```python
from contextlib import ExitStack

import concourse.bass as bass
from concourse import mybir

F32 = mybir.dt.float32
F32R = mybir.dt.float32r
ACT = mybir.ActivationFunctionType
ALU = mybir.AluOpType
AX = mybir.AxisListType

P = 128
GRAPHS = 128
G = 4
TOK = G * P
TILES = GRAPHS // G
E = 8
H = 256
HC = H // P
EPS = 1e-5
SLOTS = 4
LAG = 3



def wait(engine, sem, count):
    if not isinstance(count, int) or count > 0:
        engine.wait_ge(sem, count)


def inside(n):
    return not isinstance(n, int) or 0 <= n < TILES


def at_most(n, most):
    return min(n, most) if isinstance(n, int) else n


def every_tile(engine, tile):
    for i in range(-3, SLOTS):
        tile(i, i % SLOTS)
    with engine.Fori(SLOTS, TILES - 2 * SLOTS + 1, SLOTS) as first:
        for j in range(SLOTS):
            tile(first + j, j)
    for i in range(TILES - SLOTS, TILES + 1):
        tile(i, i % SLOTS)


def gnn_moe(nc, x, adj, w_msg, w_upd, gnn_bias, gate_w, gate_b, w1, b1, w2, b2, out, cw_dram):
    x_t = x.rearrange("(t g) n f -> t n g f", g=G)
    adj_t = adj.rearrange("(t g) i j -> t i g j", g=G)
    out_t = out.rearrange("(t g) n f -> t n g f", g=G)

    ctx = ExitStack()
    with ctx:
        def sb(name, shape, dt=F32):
            return ctx.enter_context(nc.sbuf_tensor(name, shape, dt))

        def pb(name, shape):
            return ctx.enter_context(nc.psum_tensor(name, shape, F32))

        def sem(name):
            return ctx.enter_context(nc.semaphore(name))

        w1_raw = sb("w1_raw", [P, E, H])
        w2_raw = sb("w2_raw", [P, E * HC, P])
        w1_hi = sb("w1_hi", [P, E, H], F32R)
        w1_lo = sb("w1_lo", [P, E, H], F32R)
        w2_hi = sb("w2_hi", [P, E * HC, P], F32R)
        w2_lo = sb("w2_lo", [P, E * HC, P], F32R)
        w_gnn = sb("w_gnn", [P, 2 * P])
        bias_rows = sb("bias_rows", [P, P])
        gate_raw = sb("gate_raw", [P, E])
        gate_hi = sb("gate_hi", [P, E], F32R)
        gate_lo = sb("gate_lo", [P, E], F32R)
        gate_b_rows = sb("gate_b_rows", [P, E])
        b1_cols = sb("b1_cols", [P, E * HC])
        b2_cols = sb("b2_cols", [P, E])
        ident = sb("ident", [P, P])
        ones = sb("ones", [P, 1])
        euler = sb("euler", [P, G, E])
        neg_half = sb("neg_half", [P, G])
        rank = sb("rank", [P, G, E])

        xs = sb("xs", [P, SLOTS, G, P])
        adjs = sb("adjs", [P, SLOTS, G, P])
        stats1 = sb("stats1", [P, G, 6])
        mean1 = sb("mean1", [P, G])
        var1 = sb("var1", [P, G])
        rstd1 = sb("rstd1", [P, G])
        xn1 = sb("xn1", [P, G, P])
        xn1_t = sb("xn1_t", [P, G, P])
        msg_rows = sb("msg_rows", [P, G, P])
        upd_bias = sb("upd_bias", [P, G, P])
        deg_max = sb("deg_max", [P, G])
        deg_pos = sb("deg_pos", [P, G])
        deg_inv = sb("deg_inv", [P, G])
        deg_scale = sb("deg_scale", [P, G])
        pre_relu = sb("pre_relu", [P, G, P])
        x2 = sb("x2", [P, SLOTS, G, P])
        stats2 = sb("stats2", [P, G, 6])
        mean2 = sb("mean2", [P, G])
        var2 = sb("var2", [P, G])
        rstd2 = sb("rstd2", [P, G])
        xn2 = sb("xn2", [P, G, P])
        xt_hi = sb("xt_hi", [P, SLOTS, TOK], F32R)
        xt_lo = sb("xt_lo", [P, SLOTS, TOK], F32R)

        mean_gap = sb("mean_gap", [P, G])
        mean_sum = sb("mean_sum", [P, G])
        sq_sum = sb("sq_sum", [P, G])
        gap_sq = sb("gap_sq", [P, G])
        sq_all = sb("sq_all", [P, G])

        logits = sb("logits", [P, G, E])
        top_logit = sb("top_logit", [P, G])
        below_top = sb("below_top", [P, G, E])
        powers = sb("powers", [P, G, E])
        total = sb("total", [P, G])
        inv_total = sb("inv_total", [P, G])
        probs = sb("probs", [P, G, E])
        best = sb("best", [P, 2, G])
        ties = sb("ties", [P, 2, G, E])
        keys = sb("keys", [P, 2, G, E])
        key = sb("key", [P, 2, G])
        chosen = sb("chosen", [P, 2, G, E])
        rest = sb("rest", [P, G, E])
        both = sb("both", [P, G, E])
        cw = sb("cw", [P, G, E])
        cw_t = sb("cw_t", [E, 2, TOK])
        cw_rows = sb("cw_rows", [P, 2, E, TOK])

        gel = sb("gel", [P, 2, HC, TOK])
        gel_hi = sb("gel_hi", [P, 4, HC, TOK], F32R)
        gel_lo = sb("gel_lo", [P, 4, HC, TOK], F32R)
        weighted = sb("weighted", [P, 4, TOK])
        acc = sb("acc", [P, 2, TOK])
        result = sb("result", [P, 2, G, P])

        ps_hid = pb("ps_hid", [P, HC, TOK])
        ps_y = pb("ps_y", [P, 2, TOK])
        ps_gnn = pb("ps_gnn", [P, G, 2 * P])
        ps_t = pb("ps_t", [P, G, P])
        ps_s = pb("ps_s", [P, TOK])

        consts_in = sem("consts_in")
        w_in = sem("w_in")
        w_hi_ready = sem("w_hi_ready")
        w_ready = sem("w_ready")
        blank = sem("blank")
        consts_ready = sem("consts_ready")
        x_in = [sem(f"x_in{j}") for j in range(SLOTS)]
        adj_in = [sem(f"adj_in{j}") for j in range(SLOTS)]
        stats1_step = sem("stats1_step")
        rstd1_ready = sem("rstd1_ready")
        xn1_ready = sem("xn1_ready")
        xn1_t_done = sem("xn1_t_done")
        xn1_t_ready = sem("xn1_t_ready")
        gnn_done = sem("gnn_done")
        msg_ready = sem("msg_ready")
        upd_ready = sem("upd_ready")
        agg_done = sem("agg_done")
        deg_step = sem("deg_step")
        pre_relu_ready = sem("pre_relu_ready")
        x2_ready = sem("x2_ready")
        stats2_step = sem("stats2_step")
        rstd2_ready = sem("rstd2_ready")
        xn2_ready = sem("xn2_ready")
        xn2_t_done = sem("xn2_t_done")
        xt_hi_ready = sem("xt_hi_ready")
        xt_ready = sem("xt_ready")
        gate_done = sem("gate_done")
        below_step = sem("below_step")
        powers_ready = sem("powers_ready")
        route_step = sem("route_step")
        route_choice = sem("route_choice")
        cw_t_done = sem("cw_t_done")
        cw_t_ready = sem("cw_t_ready")
        cw_stored = [sem(f"cw_stored{j}") for j in range(2)]
        cw_in = [sem(f"cw_in{j}") for j in range(2)]
        hid_done = sem("hid_done")
        gel_done = sem("gel_done")
        gel_hi_ready = sem("gel_hi_ready")
        gel_ready = sem("gel_ready")
        y_done = sem("y_done")
        y_used = sem("y_used")
        added = sem("added")
        result_t_done = sem("result_t_done")
        result_ready = sem("result_ready")
        out_stored = [sem(f"out_stored{j}") for j in range(2)]

        STATS = 6
        ROUTE = 14
        DEG = 4
        BELOW = 3

        block = ctx.enter_context(nc.Block())

        @block.sync
        def _(sp):
            def load_x(n, j):
                wait(sp, x2_ready, n - SLOTS + 1)
                sp.dma_start(xs[:, j], x_t[n]).then_inc(x_in[j], 16)

            load_x(0, 0)
            sp.dma_start(w_gnn[:, 0:P], w_msg).then_inc(consts_in, 16)
            sp.dma_start(w_gnn[:, P:], w_upd).then_inc(consts_in, 16)
            sp.dma_start(bias_rows[:], gnn_bias.partition_broadcast(P)).then_inc(consts_in, 16)
            load_x(1, 1)
            sp.dma_start(gate_raw[:], gate_w).then_inc(consts_in, 16)
            sp.dma_start(gate_b_rows[:], gate_b.partition_broadcast(P)).then_inc(consts_in, 16)
            sp.dma_start(w1_raw[:], w1.rearrange("e d h -> d e h")).then_inc(w_in, 16)
            sp.dma_start(w2_raw[:], w2.rearrange("e (c h) d -> h (e c) d", c=HC)).then_inc(w_in, 16)
            with nc.allow_non_contiguous_dma(reason="12 KB of biases, once"):
                sp.dma_start(b1_cols[:], b1.rearrange("e (c h) -> h (e c)", c=HC)).then_inc(consts_in, 16)
                sp.dma_start(b2_cols[:], b2.rearrange("e d -> d e")).then_inc(consts_in, 16)
            load_x(2, 2)
            load_x(3, 3)

            def tile(i, j):
                if inside(i) and inside(i + SLOTS):
                    load_x(i + SLOTS, j)
                if inside(i - 1):
                    sp.wait_ge(result_ready, i)
                    sp.dma_start(out_t[i - 1], result[:, (j - 1) % 2]).then_inc(out_stored[(j - 1) % 2], 16)
                if inside(i + 1):
                    n, k = i + 1, (j + 1) % 2
                    sp.compute_val(n + 1)
                    sp.compute_val(E * (n - 1))
                    sp.wait_ge(cw_t_ready, n + 1)
                    sp.dma_start(cw_dram[n], cw_t[:, k]).then_inc(cw_stored[k], 16)
                    sp.wait_ge(cw_stored[k], 16 * (n // 2 + 1) if isinstance(n, int) else 8 * (n - k) + 16)
                    wait(sp, y_used, E * (n - 1))
                    sp.dma_start(cw_rows[:, k].rearrange("p e t -> p (e t)"),
                                 cw_dram[n].rearrange("e t -> (e t)").partition_broadcast(P))\
                      .then_inc(cw_in[k], 16)

            every_tile(sp, tile)
            for k in range(2):
                sp.wait_ge(out_stored[k], 16 * (TILES // 2))

        @block.gpsimd
        def _(pool):
            def load_adj(n, j):
                wait(pool, agg_done, n - SLOTS + 1)
                pool.dma_start(adjs[:, j], adj_t[n]).then_inc(adj_in[j], 16)

            for j in range(SLOTS):
                load_adj(j, j)
            nc.gpsimd.memset(neg_half[:], -0.5)
            nc.gpsimd.memset(ident[:], 0.0).then_inc(blank, 1)
            nc.gpsimd.memset(ones[:], 1.0)
            nc.gpsimd.memset(euler[:], 2.718281828459045)
            for e in range(E):
                nc.gpsimd.memset(rank[:, :, e:e + 1], float(E - e))
            pool.wait_ge(blank, 1)
            nc.gpsimd.affine_select(out=ident[:], in_=ident[:], compare_op=ALU.not_equal, fill=1.0, base=0,
                                    pattern=[[-1, P]], channel_multiplier=1).then_inc(consts_ready, 1)
            pool.wait_ge(consts_ready, 1)

            def inverse_deviation(n, stats_step, var, ready, rstd):
                pool.wait_ge(stats_step, STATS * (n + 1))
                nc.gpsimd.tensor_tensor(rstd[:], var[:], neg_half[:], ALU.pow).then_inc(ready, 1)

            def add(n, j, e):
                pool.wait_ge(y_used, E * n + e + 1)
                if e > 1:
                    pool.wait_ge(added, (E - 1) * n + e - 1)
                nc.gpsimd.tensor_tensor(acc[:, j % 2], acc[:, j % 2], weighted[:, e % 4], ALU.add).then_inc(added, 1)

            def tile(i, j):
                for s in range(E):
                    if s == 1 and inside(i + 1):
                        pool.wait_ge(below_step, BELOW * (i + 2))
                        wait(pool, route_step, ROUTE * (i + 1))
                        nc.gpsimd.tensor_tensor(powers[:], euler[:], below_top[:], ALU.pow).then_inc(powers_ready, 1)
                    if s == 0 and inside(i) and inside(i + SLOTS):
                        load_adj(i + SLOTS, j)
                    if s == 5 and inside(i + 2):
                        inverse_deviation(i + 2, stats2_step, var2, rstd2_ready, rstd2)
                    if s == 7 and inside(i + 3):
                        inverse_deviation(i + 3, stats1_step, var1, rstd1_ready, rstd1)
                    e = (s - LAG) % E
                    n, k = (i, j) if s >= LAG else (i - 1, j - 1)
                    if inside(n) and e > 0:
                        add(n, k, e)

            every_tile(pool, tile)

        @block.scalar
        def _(act):
            act.wait_ge(consts_in, 7 * 16)
            nc.scalar.activation(gate_hi[:], gate_raw[:], ACT.Copy).then_inc(w_hi_ready, 1)
            act.wait_ge(w_in, 2 * 16)
            nc.scalar.activation(w1_hi[:], w1_raw[:], ACT.Copy).then_inc(w_hi_ready, 1)
            nc.scalar.activation(w2_hi[:], w2_raw[:], ACT.Copy).then_inc(w_hi_ready, 1)

            def tile(i, j):
                for s in range(E):
                    if s == 1 and inside(i + 2):
                        n = i + 2
                        act.wait_ge(xn1_t_done, n + 1)
                        wait(act, gnn_done, n)
                        nc.scalar.activation(xn1_t[:], ps_t[:], ACT.Copy).then_inc(xn1_t_ready, 1)
                    if s == 2 and inside(i + 2):
                        n = i + 2
                        act.wait_ge(gnn_done, n + 1)
                        wait(act, agg_done, n)
                        nc.scalar.activation(msg_rows[:], ps_gnn[:, :, 0:P], ACT.Copy).then_inc(msg_ready, 1)
                    if s == 6 and inside(i + 1):
                        n, k = i + 1, (j + 1) % 2
                        act.wait_ge(cw_t_done, n + 1)
                        wait(act, cw_stored[k], 16 * (n // 2) if isinstance(n, int) else 8 * (n - k))
                        nc.scalar.activation(cw_t[:, k], ps_s[0:E, :], ACT.Copy).then_inc(cw_t_ready, 1)
                    if s == 7 and inside(i + 2):
                        act.wait_ge(xn2_t_done, i + 3)
                        nc.scalar.activation(xt_hi[:, (j + 2) % SLOTS], ps_t[:].rearrange("p g t -> p (g t)"),
                                             ACT.Copy).then_inc(xt_hi_ready, 1)
                    if inside(i):
                        ex = E * i + s
                        wait(act, gel_ready, ex - 1)
                        for c in range(HC):
                            act.wait_ge(hid_done, HC * ex + c + 1)
                            nc.scalar.activation(gel[:, s % 2, c], ps_hid[:, c], ACT.Gelu,
                                                 bias=b1_cols[:, HC * s + c:HC * s + c + 1]).then_inc(gel_done, 1)
                        act.wait_ge(gel_done, HC * ex + HC)
                        wait(act, y_done, ex - 3)
                        nc.scalar.activation(gel_hi[:, s % 4], gel[:, s % 2], ACT.Copy).then_inc(gel_hi_ready, 1)

            every_tile(act, tile)

        @block.vector
        def _(dve):
            dve.wait_ge(w_hi_ready, 1)
            nc.vector.tensor_tensor(gate_lo[:], gate_raw[:], gate_hi[:].bitcast(F32), ALU.subtract).then_inc(w_ready, 1)

            def split_weights():
                dve.wait_ge(w_hi_ready, 3)
                nc.vector.tensor_tensor(w1_lo[:], w1_raw[:], w1_hi[:].bitcast(F32), ALU.subtract).then_inc(w_ready, 1)
                nc.vector.tensor_tensor(w2_lo[:], w2_raw[:], w2_hi[:].bitcast(F32), ALU.subtract).then_inc(w_ready, 1)

            def statistics(n, rows, step, stats, mean, var):
                for g in range(G):
                    last = nc.vector.bn_stats(stats[:, g], rows[:, g])
                last.then_inc(step, 1)
                half, mean_e, mean_o, sq_e, sq_o = P // 2, stats[:, :, 1], stats[:, :, 4], stats[:, :, 2], stats[:, :, 5]
                dve.wait_ge(step, STATS * n + 1)
                nc.vector.tensor_tensor(mean_gap[:], mean_e, mean_o, ALU.subtract).then_inc(step, 1)
                nc.vector.tensor_tensor(mean_sum[:], mean_e, mean_o, ALU.add).then_inc(step, 1)
                nc.vector.tensor_tensor(sq_sum[:], sq_e, sq_o, ALU.add)
                dve.wait_ge(step, STATS * n + 2)
                nc.vector.scalar_tensor_tensor(gap_sq[:], mean_gap[:], half / 2.0, mean_gap[:], ALU.mult, ALU.mult)\
                  .then_inc(step, 1)
                dve.wait_ge(step, STATS * n + 3)
                nc.vector.tensor_scalar(mean[:], mean_sum[:], 0.5, None, ALU.mult)
                dve.wait_ge(step, STATS * n + 4)
                nc.vector.tensor_tensor(sq_all[:], sq_sum[:], gap_sq[:], ALU.add).then_inc(step, 1)
                dve.wait_ge(step, STATS * n + 5)
                nc.vector.tensor_scalar(var[:], sq_all[:], 1.0 / P, EPS, ALU.mult, ALU.add).then_inc(step, 1)

            def normalise(rows, mean, rstd, normed):
                for g in range(G):
                    last = nc.vector.tensor_scalar(normed[:, g], rows[:, g], mean[:, g:g + 1], rstd[:, g:g + 1],
                                                   ALU.subtract, ALU.mult)
                return last

            def over_experts(column):
                return column.unsqueeze(2).to_broadcast([P, G, E])

            def below_maximum(n):
                dve.wait_ge(gate_done, n + 1)
                nc.vector.tensor_tensor(logits[:], ps_s[:, 0:G * E].rearrange("p (g e) -> p g e", e=E),
                                        gate_b_rows[:].unsqueeze(1).to_broadcast([P, G, E]),
                                        ALU.add).then_inc(below_step, 1)
                dve.wait_ge(below_step, BELOW * n + 1)
                nc.vector.tensor_reduce(top_logit[:], logits[:], AX.X, ALU.max).then_inc(below_step, 1)
                dve.wait_ge(below_step, BELOW * n + 2)
                nc.vector.tensor_tensor(below_top[:], logits[:], over_experts(top_logit[:]),
                                        ALU.subtract).then_inc(below_step, 1)

            def choose(n, k, p, base):
                nc.vector.tensor_reduce(best[:, k], p[:], AX.X, ALU.max).then_inc(route_step, 1)
                dve.wait_ge(route_step, ROUTE * n + base + 1)
                nc.vector.tensor_tensor(ties[:, k], p[:], over_experts(best[:, k]), ALU.is_equal).then_inc(route_step, 1)
                dve.wait_ge(route_step, ROUTE * n + base + 2)
                nc.vector.tensor_tensor(keys[:, k], ties[:, k], rank[:], ALU.mult).then_inc(route_step, 1)
                dve.wait_ge(route_step, ROUTE * n + base + 3)
                nc.vector.tensor_reduce(key[:, k], keys[:, k], AX.X, ALU.max).then_inc(route_step, 1)
                dve.wait_ge(route_step, ROUTE * n + base + 4)
                return nc.vector.tensor_tensor(chosen[:, k], keys[:, k], over_experts(key[:, k]), ALU.is_equal)

            def route(n):
                dve.wait_ge(powers_ready, n + 1)
                nc.vector.tensor_reduce(total[:], powers[:], AX.X, ALU.add).then_inc(route_step, 1)
                dve.wait_ge(route_step, ROUTE * n + 1)
                nc.vector.reciprocal(inv_total[:], total[:]).then_inc(route_step, 1)
                dve.wait_ge(route_step, ROUTE * n + 2)
                nc.vector.tensor_tensor(probs[:], powers[:], over_experts(inv_total[:]), ALU.mult).then_inc(route_step, 1)
                dve.wait_ge(route_step, ROUTE * n + 3)
                choose(n, 0, probs, 3).then_inc(route_step, 1)
                dve.wait_ge(route_step, ROUTE * n + 8)
                nc.vector.scalar_tensor_tensor(rest[:], chosen[:, 0], -2.0, probs[:], ALU.mult, ALU.add)\
                  .then_inc(route_step, 1)
                dve.wait_ge(route_step, ROUTE * n + 9)
                choose(n, 1, rest, 9).then_inc(route_choice, 1)
                dve.wait_ge(route_choice, 2 * n + 1)
                nc.vector.tensor_tensor(both[:], chosen[:, 0], chosen[:, 1], ALU.add).then_inc(route_choice, 1)
                dve.wait_ge(route_choice, 2 * n + 2)
                wait(dve, cw_t_done, n)
                nc.vector.tensor_tensor(cw[:], both[:], probs[:], ALU.mult).then_inc(route_step, 1)

            def graph_output(n, j):
                dve.wait_ge(agg_done, n + 1)
                deg = ps_s[:, 0:G]
                nc.vector.tensor_scalar(deg_max[:], deg, 1.0, None, ALU.max).then_inc(deg_step, 1)
                nc.vector.tensor_scalar(deg_pos[:], deg, 0.0, None, ALU.is_gt).then_inc(deg_step, 1)
                dve.wait_ge(deg_step, DEG * n + 1)
                nc.vector.reciprocal(deg_inv[:], deg_max[:]).then_inc(deg_step, 1)
                dve.wait_ge(deg_step, DEG * n + 3)
                nc.vector.tensor_tensor(deg_scale[:], deg_inv[:], deg_pos[:], ALU.mult).then_inc(deg_step, 1)
                dve.wait_ge(deg_step, DEG * n + 4)
                for g in range(G):
                    last = nc.vector.scalar_tensor_tensor(pre_relu[:, g], ps_gnn[:, g, 0:P], deg_scale[:, g:g + 1],
                                                          upd_bias[:, g], ALU.mult, ALU.add)
                last.then_inc(pre_relu_ready, 1)
                dve.wait_ge(pre_relu_ready, n + 1)
                nc.vector.scalar_tensor_tensor(x2[:, j], pre_relu[:], 0.0, xs[:, j], ALU.max, ALU.add)\
                  .then_inc(x2_ready, 1)

            def weigh(n, j, e):
                if e == 0:
                    dve.wait_ge(cw_in[j % 2], 16 * (n // 2 + 1) if isinstance(n, int) else 8 * (n - j % 2) + 16)
                    wait(dve, result_t_done, n - 1)
                    to = acc[:, j % 2]
                else:
                    wait(dve, added, (E - 1) * n + e - (4 if e > 4 else 7 if e == 4 else 3))
                    to = weighted[:, e % 4]
                dve.wait_ge(y_done, E * n + e + 1)
                nc.vector.scalar_tensor_tensor(to, ps_y[:, e % 2], b2_cols[:, e:e + 1], cw_rows[:, j % 2, e],
                                               ALU.add, ALU.mult).then_inc(y_used, 1)

            def tile(i, j):
                j2, j3 = (j + 2) % SLOTS, (j + 3) % SLOTS
                for s in range(E):
                    e = (s - LAG) % E
                    n, k = (i, j) if s >= LAG else (i - 1, (j - 1) % SLOTS)
                    if inside(n):
                        weigh(n, k, e)
                    if inside(i):
                        ex = E * i + s
                        dve.wait_ge(gel_hi_ready, ex + 1)
                        nc.vector.tensor_tensor(gel_lo[:, s % 4], gel[:, s % 2], gel_hi[:, s % 4].bitcast(F32),
                                                ALU.subtract).then_inc(gel_ready, 1)
                    if s == 0 and inside(i + 2):
                        dve.wait_ge(rstd1_ready, i + 3)
                        wait(dve, xn1_t_done, i + 2)
                        normalise(xs[:, j2], mean1, rstd1, xn1).then_inc(xn1_ready, 1)
                    if s == 1 and inside(i + 1):
                        below_maximum(i + 1)
                    if s == 2 and inside(i + 2):
                        dve.wait_ge(msg_ready, i + 3)
                        nc.vector.tensor_tensor(upd_bias[:], ps_gnn[:, :, P:],
                                                bias_rows[:].unsqueeze(1).to_broadcast([P, G, P]),
                                                ALU.add).then_inc(upd_ready, 1)
                    if s == 3 and inside(i + 2):
                        graph_output(i + 2, j2)
                    if s == 4 and inside(i + 1):
                        route(i + 1)
                    if s == 5 and inside(i + 2):
                        dve.wait_ge(x2_ready, i + 3)
                        statistics(i + 2, x2[:, j2], stats2_step, stats2, mean2, var2)
                    if s == 6 and inside(i - 1):
                        m, q = i - 1, (j - 1) % SLOTS
                        dve.wait_ge(result_t_done, m + 1)
                        wait(dve, out_stored[q % 2], 16 * (m // 2) if isinstance(m, int) else 8 * (m - q % 2))
                        nc.vector.tensor_tensor(result[:, q % 2], ps_t[:], x2[:, q], ALU.add).then_inc(result_ready, 1)
                    if s == 6 and inside(i + 2):
                        dve.wait_ge(rstd2_ready, i + 3)
                        wait(dve, xn2_t_done, i + 2)
                        normalise(x2[:, j2], mean2, rstd2, xn2).then_inc(xn2_ready, 1)
                    if s == 7 and inside(i + 2):
                        dve.wait_ge(xt_hi_ready, i + 3)
                        nc.vector.tensor_tensor(xt_lo[:, j2], ps_t[:].rearrange("p g t -> p (g t)"),
                                                xt_hi[:, j2].bitcast(F32), ALU.subtract).then_inc(xt_ready, 1)
                    if s == 7 and inside(i + 3):
                        m = i + 3
                        dve.wait_ge(x_in[j3], 16 * (m // SLOTS + 1) if isinstance(m, int) else 4 * (m - j3) + 16)
                        statistics(m, xs[:, j3], stats1_step, stats1, mean1, var1)
                if isinstance(i, int) and i == -2:
                    split_weights()

            dve.wait_ge(consts_in, 7 * 16)
            dve.wait_ge(consts_ready, 1)
            every_tile(dve, tile)

        @block.tensor
        def _(pe):
            pe.wait_ge(consts_in, 7 * 16)
            pe.wait_ge(consts_ready, 1)

            def first_product(n, j, e):
                ex = E * n + e
                for c in range(HC):
                    wait(pe, gel_done, HC * (ex - 1) + c + 1)
                    cols = slice(c * P, c * P + P)
                    nc.tensor.matmul(ps_hid[:, c], w1_hi[:, e, cols], xt_hi[:, j], start=True, stop=False)
                    nc.tensor.matmul(ps_hid[:, c], w1_hi[:, e, cols], xt_lo[:, j], start=False, stop=False)
                    nc.tensor.matmul(ps_hid[:, c], w1_lo[:, e, cols], xt_hi[:, j], start=False, stop=True)\
                      .then_inc(hid_done, 1)

            def second_product(n, e):
                ex = E * n + e
                pe.wait_ge(gel_ready, ex + 1)
                wait(pe, y_used, ex - 1)
                for c in range(HC):
                    w = HC * e + c
                    nc.tensor.matmul(ps_y[:, e % 2], w2_hi[:, w], gel_hi[:, e % 4, c], start=c == 0, stop=False)
                    nc.tensor.matmul(ps_y[:, e % 2], w2_hi[:, w], gel_lo[:, e % 4, c], start=False, stop=False)
                    last = nc.tensor.matmul(ps_y[:, e % 2], w2_lo[:, w], gel_hi[:, e % 4, c],
                                            start=False, stop=c == HC - 1)
                last.then_inc(y_done, 1)

            def tile(i, j):
                j2 = (j + 2) % SLOTS
                if isinstance(i, int) and i == 0:
                    pe.wait_ge(w_ready, 3)
                for s in range(E):
                    if s == 0 and inside(i + 1):
                        n, k = i + 1, (j + 1) % SLOTS
                        pe.wait_ge(xt_ready, n + 1)
                        pe.wait_ge(w_ready, 1)
                        wait(pe, cw_t_ready, n)
                        for g in range(G):
                            at = slice(g * P, g * P + P)
                            to = ps_s[:, g * E:g * E + E]
                            nc.tensor.matmul(to, xt_hi[:, k, at], gate_hi[:], start=True, stop=False)
                            nc.tensor.matmul(to, xt_lo[:, k, at], gate_hi[:], start=False, stop=False)
                            last = nc.tensor.matmul(to, xt_hi[:, k, at], gate_lo[:], start=False, stop=True)
                        last.then_inc(gate_done, 1)
                    if s == 1 and inside(i + 2):
                        n = i + 2
                        pe.wait_ge(xn1_ready, n + 1)
                        wait(pe, xt_ready, n)
                        for g in range(G):
                            last = nc.tensor.transpose(ps_t[:, g], xn1[:, g], ident[:])
                        last.then_inc(xn1_t_done, 1)
                    if s == 2 and inside(i + 2):
                        n = i + 2
                        pe.wait_ge(xn1_t_ready, n + 1)
                        wait(pe, pre_relu_ready, n)
                        for g in range(G):
                            last = nc.tensor.matmul(ps_gnn[:, g], xn1_t[:, g], w_gnn[:], start=True, stop=True)
                        last.then_inc(gnn_done, 1)
                    if s == 3 and inside(i + 2):
                        n = i + 2
                        pe.wait_ge(adj_in[j2], 16 * (n // SLOTS + 1) if isinstance(n, int) else 4 * (n - j2) + 16)
                        pe.wait_ge(upd_ready, n + 1)
                        wait(pe, below_step, BELOW * (n - 1) + 1)
                        for g in range(G):
                            nc.tensor.matmul(ps_gnn[:, g, 0:P], adjs[:, j2, g], msg_rows[:, g], start=True, stop=True)
                            last = nc.tensor.matmul(ps_s[:, g:g + 1], adjs[:, j2, g], ones[:], start=True, stop=True)
                        last.then_inc(agg_done, 1)
                    if s == 6 and inside(i - 1):
                        n, k = i - 1, (j - 1) % 2
                        pe.wait_ge(added, (E - 1) * (n + 1))
                        pe.wait_ge(xn1_t_ready, at_most(i + 3, TILES))
                        wait(pe, result_ready, n)
                        for g in range(G):
                            last = nc.tensor.transpose(ps_t[:, g], acc[:, k, g * P:g * P + P], ident[:])
                        last.then_inc(result_t_done, 1)
                    if s == 6 and inside(i + 1):
                        n = i + 1
                        pe.wait_ge(route_step, ROUTE * (n + 1))
                        pe.wait_ge(deg_step, at_most(DEG * (n + 1) + 2, DEG * TILES))
                        for g in range(G):
                            last = nc.tensor.transpose(ps_s[0:E, g * P:g * P + P], cw[:, g], ident[:])
                        last.then_inc(cw_t_done, 1)
                    if s == 7 and inside(i + 2):
                        n = i + 2
                        pe.wait_ge(xn2_ready, n + 1)
                        wait(pe, result_ready, i)
                        for g in range(G):
                            last = nc.tensor.transpose(ps_t[:, g], xn2[:, g], ident[:])
                        last.then_inc(xn2_t_done, 1)
                    if inside(i):
                        first_product(i, j, s)
                    e = (s - LAG) % E
                    n = i if s >= LAG else i - 1
                    if inside(n):
                        second_product(n, e)

            every_tile(pe, tile)


_INS = ["x", "adj", "L0_gnn_W_msg", "L0_gnn_W_upd", "L0_gnn_bias", "L0_ffn_gate_w", "L0_ffn_gate_b",
        "L0_ffn_W1", "L0_ffn_b1", "L0_ffn_W2", "L0_ffn_b2"]


def kernel(**inputs):
    import numpy as np
    import concourse.bacc as bacc
    from concourse.bass_utils import run_bass_kernel_spmd as run

    nc = bacc.Bacc("TRN2", target_bir_lowering=False, num_devices=1)
    arrays, args = {}, []
    for name in _INS:
        a = np.ascontiguousarray(inputs[name])
        arrays[f"in_{name}"] = a
        args.append(nc.dram_tensor(f"in_{name}", a.shape, mybir.dt.from_np(a.dtype), kind="ExternalInput").ap())
    out = nc.dram_tensor("out", (GRAPHS, P, P), F32, kind="ExternalOutput").ap()
    cw_dram = nc.dram_tensor("cw_dram", (TILES, E, TOK), F32, kind="Internal").ap()
    gnn_moe(nc, *args, out, cw_dram)
    return run(nc, [arrays], core_ids=[0]).results[0]["out"]
```

```python
from contextlib import ExitStack

import concourse.bass as bass
from concourse import mybir

F32 = mybir.dt.float32
F32R = mybir.dt.float32r
ACT = mybir.ActivationFunctionType
ALU = mybir.AluOpType
AX = mybir.AxisListType

P = 128
GRAPHS = 128
G = 4
TOK = G * P
TILES = GRAPHS // G
E = 8
H = 256
HC = H // P
EPS = 1e-5
SLOTS = 4
LAG = 3



def wait(engine, sem, count):
    if not isinstance(count, int) or count > 0:
        engine.wait_ge(sem, count)


def inside(n):
    return not isinstance(n, int) or 0 <= n < TILES


def at_most(n, most):
    return min(n, most) if isinstance(n, int) else n


def every_tile(engine, tile):
    for i in range(-3, SLOTS):
        tile(i, i % SLOTS)
    with engine.Fori(SLOTS, TILES - 2 * SLOTS + 1, SLOTS) as first:
        for j in range(SLOTS):
            tile(first + j, j)
    for i in range(TILES - SLOTS, TILES + 1):
        tile(i, i % SLOTS)


def gnn_moe(nc, x, adj, w_msg, w_upd, gnn_bias, gate_w, gate_b, w1, b1, w2, b2, out, cw_dram):
    x_t = x.rearrange("(t g) n f -> t n g f", g=G)
    adj_t = adj.rearrange("(t g) i j -> t i g j", g=G)
    out_t = out.rearrange("(t g) n f -> t n g f", g=G)

    ctx = ExitStack()
    with ctx:
        def sb(name, shape, dt=F32):
            return ctx.enter_context(nc.sbuf_tensor(name, shape, dt))

        def pb(name, shape):
            return ctx.enter_context(nc.psum_tensor(name, shape, F32))

        def sem(name):
            return ctx.enter_context(nc.semaphore(name))

        w1_raw = sb("w1_raw", [P, E, H])
        w2_raw = sb("w2_raw", [P, E * HC, P])
        w1_hi = sb("w1_hi", [P, E, H], F32R)
        w1_lo = sb("w1_lo", [P, E, H], F32R)
        w2_hi = sb("w2_hi", [P, E * HC, P], F32R)
        w2_lo = sb("w2_lo", [P, E * HC, P], F32R)
        w_gnn = sb("w_gnn", [P, 2 * P])
        bias_rows = sb("bias_rows", [P, P])
        gate_raw = sb("gate_raw", [P, E])
        gate_hi = sb("gate_hi", [P, E], F32R)
        gate_lo = sb("gate_lo", [P, E], F32R)
        gate_b_rows = sb("gate_b_rows", [P, E])
        b1_cols = sb("b1_cols", [P, E * HC])
        b2_cols = sb("b2_cols", [P, E])
        ident = sb("ident", [P, P])
        euler = sb("euler", [P, G, E])
        neg_half = sb("neg_half", [P, G])
        rank = sb("rank", [P, G, E])

        xs = sb("xs", [P, SLOTS, G, P])
        adjs = sb("adjs", [P, SLOTS, G, P])
        stats1 = sb("stats1", [P, G, 6])
        mean1 = sb("mean1", [P, G])
        var1 = sb("var1", [P, G])
        rstd1 = sb("rstd1", [P, G])
        xn1 = sb("xn1", [P, G, P])
        xn1_t = sb("xn1_t", [P, G, P])
        msg_rows = sb("msg_rows", [P, G, P + 1])
        upd_bias = sb("upd_bias", [P, G, P])
        deg_max = sb("deg_max", [P, G])
        deg_pos = sb("deg_pos", [P, G])
        deg_inv = sb("deg_inv", [P, G])
        deg_scale = sb("deg_scale", [P, G])
        pre_relu = sb("pre_relu", [P, G, P])
        x2 = sb("x2", [P, SLOTS, G, P])
        stats2 = sb("stats2", [P, G, 6])
        mean2 = sb("mean2", [P, G])
        var2 = sb("var2", [P, G])
        rstd2 = sb("rstd2", [P, G])
        xn2 = sb("xn2", [P, G, P])
        xt_hi = sb("xt_hi", [P, SLOTS, TOK], F32R)
        xt_lo = sb("xt_lo", [P, SLOTS, TOK], F32R)

        mean_gap = sb("mean_gap", [P, G])
        mean_sum = sb("mean_sum", [P, G])
        sq_sum = sb("sq_sum", [P, G])
        gap_sq = sb("gap_sq", [P, G])
        sq_all = sb("sq_all", [P, G])

        logits = sb("logits", [P, G, E])
        top_logit = sb("top_logit", [P, G])
        below_top = sb("below_top", [P, G, E])
        powers = sb("powers", [P, G, E])
        total = sb("total", [P, G])
        inv_total = sb("inv_total", [P, G])
        keys = sb("keys", [P, 2, G, E])
        key = sb("key", [P, 2, G])
        chosen = sb("chosen", [P, 2, G, E])
        rest = sb("rest", [P, G, E])
        best_rest = sb("best_rest", [P, G])
        below_best = sb("below_best", [P, G, E])
        both = sb("both", [P, G, E])
        kept = sb("kept", [P, G, E])
        cw = sb("cw", [P, G, E])
        cw_t = sb("cw_t", [E, 2, TOK])
        cw_rows = sb("cw_rows", [P, 2, E, TOK])

        gel = sb("gel", [P, 2, HC, TOK])
        gel_hi = sb("gel_hi", [P, 4, HC, TOK], F32R)
        gel_lo = sb("gel_lo", [P, 4, HC, TOK], F32R)
        weighted = sb("weighted", [P, 4, TOK])
        acc = sb("acc", [P, 2, TOK])
        result = sb("result", [P, 2, G, P])

        ps_hid = pb("ps_hid", [P, HC, TOK])
        ps_y = pb("ps_y", [P, 2, TOK])
        ps_gnn = pb("ps_gnn", [P, G, 2 * P])
        ps_t = pb("ps_t", [P, G, P])
        ps_s = pb("ps_s", [P, TOK])

        xn1_ps = ps_gnn[:, 0:2].rearrange("p a (g t) -> p (a g) t", g=2)

        consts_in = sem("consts_in")
        w_in = sem("w_in")
        w_hi_ready = sem("w_hi_ready")
        w_ready = sem("w_ready")
        blank = sem("blank")
        consts_ready = sem("consts_ready")
        x_in = [sem(f"x_in{j}") for j in range(SLOTS)]
        adj_in = [sem(f"adj_in{j}") for j in range(SLOTS)]
        stats1_step = sem("stats1_step")
        rstd1_ready = sem("rstd1_ready")
        xn1_ready = sem("xn1_ready")
        xn1_t_done = sem("xn1_t_done")
        xn1_t_ready = sem("xn1_t_ready")
        gnn_done = sem("gnn_done")
        msg_ready = sem("msg_ready")
        upd_ready = sem("upd_ready")
        agg_done = sem("agg_done")
        deg_step = sem("deg_step")
        pre_relu_ready = sem("pre_relu_ready")
        x2_ready = sem("x2_ready")
        stats2_step = sem("stats2_step")
        rstd2_ready = sem("rstd2_ready")
        xn2_ready = sem("xn2_ready")
        xn2_t_done = sem("xn2_t_done")
        xt_hi_ready = sem("xt_hi_ready")
        xt_ready = sem("xt_ready")
        gate_done = sem("gate_done")
        below_step = sem("below_step")
        choice_step = sem("choice_step")
        powers_ready = sem("powers_ready")
        route_step = sem("route_step")
        cw_t_done = sem("cw_t_done")
        cw_t_ready = sem("cw_t_ready")
        cw_stored = [sem(f"cw_stored{j}") for j in range(2)]
        cw_in = [sem(f"cw_in{j}") for j in range(2)]
        hid_done = sem("hid_done")
        gel_done = sem("gel_done")
        gel_hi_ready = sem("gel_hi_ready")
        gel_ready = sem("gel_ready")
        y_done = sem("y_done")
        y_used = sem("y_used")
        added = sem("added")
        result_t_done = sem("result_t_done")
        result_ready = sem("result_ready")
        out_stored = [sem(f"out_stored{j}") for j in range(2)]

        STATS = 6
        DEG = 4
        BELOW = 3
        CHOICE = 10
        ROUTE = 4

        block = ctx.enter_context(nc.Block())

        @block.sync
        def _(sp):
            def load_x(n, j):
                wait(sp, x2_ready, n - SLOTS + 1)
                sp.dma_start(xs[:, j], x_t[n]).then_inc(x_in[j], 16)

            load_x(0, 0)
            sp.dma_start(w_gnn[:, 0:P], w_msg).then_inc(consts_in, 16)
            sp.dma_start(w_gnn[:, P:], w_upd).then_inc(consts_in, 16)
            sp.dma_start(bias_rows[:], gnn_bias.partition_broadcast(P)).then_inc(consts_in, 16)
            load_x(1, 1)
            sp.dma_start(gate_raw[:], gate_w).then_inc(consts_in, 16)
            sp.dma_start(gate_b_rows[:], gate_b.partition_broadcast(P)).then_inc(consts_in, 16)
            sp.dma_start(w1_raw[:], w1.rearrange("e d h -> d e h")).then_inc(w_in, 16)
            sp.dma_start(w2_raw[:], w2.rearrange("e (c h) d -> h (e c) d", c=HC)).then_inc(w_in, 16)
            with nc.allow_non_contiguous_dma(reason="12 KB of biases, once"):
                sp.dma_start(b1_cols[:], b1.rearrange("e (c h) -> h (e c)", c=HC)).then_inc(consts_in, 16)
                sp.dma_start(b2_cols[:], b2.rearrange("e d -> d e")).then_inc(consts_in, 16)
            load_x(2, 2)
            load_x(3, 3)

            def tile(i, j):
                if inside(i) and inside(i + SLOTS):
                    load_x(i + SLOTS, j)
                if inside(i - 1):
                    sp.wait_ge(result_ready, i)
                    sp.dma_start(out_t[i - 1], result[:, (j - 1) % 2]).then_inc(out_stored[(j - 1) % 2], 16)
                if inside(i + 1):
                    n, k = i + 1, (j + 1) % 2
                    sp.compute_val(n + 1)
                    sp.compute_val(E * (n - 1))
                    sp.wait_ge(cw_t_ready, n + 1)
                    sp.dma_start(cw_dram[n], cw_t[:, k]).then_inc(cw_stored[k], 16)
                    sp.wait_ge(cw_stored[k], 16 * (n // 2 + 1) if isinstance(n, int) else 8 * (n - k) + 16)
                    wait(sp, y_used, E * (n - 1))
                    sp.dma_start(cw_rows[:, k].rearrange("p e t -> p (e t)"),
                                 cw_dram[n].rearrange("e t -> (e t)").partition_broadcast(P))\
                      .then_inc(cw_in[k], 16)

            every_tile(sp, tile)
            for k in range(2):
                sp.wait_ge(out_stored[k], 16 * (TILES // 2))

        @block.gpsimd
        def _(pool):
            def load_adj(n, j):
                wait(pool, agg_done, n - SLOTS + 1)
                pool.dma_start(adjs[:, j], adj_t[n]).then_inc(adj_in[j], 16)

            for j in range(SLOTS):
                load_adj(j, j)
            nc.gpsimd.memset(neg_half[:], -0.5)
            nc.gpsimd.memset(ident[:], 0.0).then_inc(blank, 1)
            nc.gpsimd.memset(msg_rows[:, :, P:], 1.0)
            nc.gpsimd.memset(euler[:], 2.718281828459045)
            for e in range(E):
                nc.gpsimd.memset(rank[:, :, e:e + 1], float(E - e))
            pool.wait_ge(blank, 1)
            nc.gpsimd.affine_select(out=ident[:], in_=ident[:], compare_op=ALU.not_equal, fill=1.0, base=0,
                                    pattern=[[-1, P]], channel_multiplier=1).then_inc(consts_ready, 1)
            pool.wait_ge(consts_ready, 1)

            def inverse_deviation(n, stats_step, var, ready, rstd):
                pool.wait_ge(stats_step, STATS * (n + 1))
                nc.gpsimd.tensor_tensor(rstd[:], var[:], neg_half[:], ALU.pow).then_inc(ready, 1)

            def add(n, j, e):
                pool.wait_ge(y_used, E * n + e + 1)
                if e > 1:
                    pool.wait_ge(added, (E - 1) * n + e - 1)
                nc.gpsimd.tensor_tensor(acc[:, j % 2], acc[:, j % 2], weighted[:, e % 4], ALU.add).then_inc(added, 1)

            def tile(i, j):
                for s in range(E):
                    if s == 0 and inside(i + 3):
                        inverse_deviation(i + 3, stats1_step, var1, rstd1_ready, rstd1)
                    if s == 1 and inside(i + 1):
                        pool.wait_ge(below_step, BELOW * (i + 2))
                        wait(pool, route_step, ROUTE * (i + 1))
                        nc.gpsimd.tensor_tensor(powers[:], euler[:], below_top[:], ALU.pow).then_inc(powers_ready, 1)
                    if s == 4 and inside(i + 2):
                        inverse_deviation(i + 2, stats2_step, var2, rstd2_ready, rstd2)
                    if s == 6 and inside(i) and inside(i + SLOTS):
                        load_adj(i + SLOTS, j)
                    e = (s - LAG) % E
                    n, k = (i, j) if s >= LAG else (i - 1, j - 1)
                    if inside(n) and e > 0:
                        add(n, k, e)

            every_tile(pool, tile)

        @block.scalar
        def _(act):
            act.wait_ge(consts_in, 7 * 16)
            nc.scalar.activation(gate_hi[:], gate_raw[:], ACT.Copy).then_inc(w_hi_ready, 1)
            act.wait_ge(w_in, 2 * 16)
            nc.scalar.activation(w1_hi[:], w1_raw[:], ACT.Copy).then_inc(w_hi_ready, 1)
            nc.scalar.activation(w2_hi[:], w2_raw[:], ACT.Copy).then_inc(w_hi_ready, 1)

            def tile(i, j):
                for s in range(E):
                    if s == 0 and inside(i + 2):
                        n = i + 2
                        act.wait_ge(gnn_done, n + 1)
                        wait(act, agg_done, n)
                        nc.scalar.activation(msg_rows[:, :, 0:P], ps_gnn[:, :, 0:P], ACT.Copy).then_inc(msg_ready, 1)
                    if s == 5 and inside(i + 1):
                        n, k = i + 1, (j + 1) % 2
                        act.wait_ge(cw_t_done, n + 1)
                        wait(act, cw_stored[k], 16 * (n // 2) if isinstance(n, int) else 8 * (n - k))
                        nc.scalar.activation(cw_t[:, k], ps_s[0:E, :], ACT.Copy).then_inc(cw_t_ready, 1)
                    if s == 6 and inside(i + 2):
                        act.wait_ge(xn2_t_done, i + 3)
                        nc.scalar.activation(xt_hi[:, (j + 2) % SLOTS], ps_t[:].rearrange("p g t -> p (g t)"),
                                             ACT.Copy).then_inc(xt_hi_ready, 1)
                    if s == 7 and inside(i + 3):
                        n = i + 3
                        act.wait_ge(xn1_t_done, n + 1)
                        wait(act, gnn_done, n)
                        nc.scalar.activation(xn1_t[:], xn1_ps, ACT.Copy).then_inc(xn1_t_ready, 1)
                    if inside(i):
                        ex = E * i + s
                        wait(act, gel_ready, ex - 1)
                        for c in range(HC):
                            act.wait_ge(hid_done, HC * ex + c + 1)
                            nc.scalar.activation(gel[:, s % 2, c], ps_hid[:, c], ACT.Gelu,
                                                 bias=b1_cols[:, HC * s + c:HC * s + c + 1]).then_inc(gel_done, 1)
                        act.wait_ge(gel_done, HC * ex + HC)
                        wait(act, y_done, ex - 3)
                        nc.scalar.activation(gel_hi[:, s % 4], gel[:, s % 2], ACT.Copy).then_inc(gel_hi_ready, 1)

            every_tile(act, tile)

        @block.vector
        def _(dve):
            dve.wait_ge(w_hi_ready, 1)
            nc.vector.tensor_tensor(gate_lo[:], gate_raw[:], gate_hi[:].bitcast(F32), ALU.subtract).then_inc(w_ready, 1)

            def split_weights():
                dve.wait_ge(w_hi_ready, 3)
                nc.vector.tensor_tensor(w1_lo[:], w1_raw[:], w1_hi[:].bitcast(F32), ALU.subtract).then_inc(w_ready, 1)
                nc.vector.tensor_tensor(w2_lo[:], w2_raw[:], w2_hi[:].bitcast(F32), ALU.subtract).then_inc(w_ready, 1)

            def statistics(n, rows, step, stats, mean, var):
                for g in range(G):
                    last = nc.vector.bn_stats(stats[:, g], rows[:, g])
                last.then_inc(step, 1)
                half, mean_e, mean_o, sq_e, sq_o = P // 2, stats[:, :, 1], stats[:, :, 4], stats[:, :, 2], stats[:, :, 5]
                dve.wait_ge(step, STATS * n + 1)
                nc.vector.tensor_tensor(mean_gap[:], mean_e, mean_o, ALU.subtract).then_inc(step, 1)
                nc.vector.tensor_tensor(mean_sum[:], mean_e, mean_o, ALU.add).then_inc(step, 1)
                nc.vector.tensor_tensor(sq_sum[:], sq_e, sq_o, ALU.add)
                dve.wait_ge(step, STATS * n + 2)
                nc.vector.scalar_tensor_tensor(gap_sq[:], mean_gap[:], half / 2.0, mean_gap[:], ALU.mult, ALU.mult)\
                  .then_inc(step, 1)
                dve.wait_ge(step, STATS * n + 3)
                nc.vector.tensor_scalar(mean[:], mean_sum[:], 0.5, None, ALU.mult)
                dve.wait_ge(step, STATS * n + 4)
                nc.vector.tensor_tensor(sq_all[:], sq_sum[:], gap_sq[:], ALU.add).then_inc(step, 1)
                dve.wait_ge(step, STATS * n + 5)
                nc.vector.tensor_scalar(var[:], sq_all[:], 1.0 / P, EPS, ALU.mult, ALU.add).then_inc(step, 1)

            def normalise(rows, mean, rstd, normed):
                for g in range(G):
                    last = nc.vector.tensor_scalar(normed[:, g], rows[:, g], mean[:, g:g + 1], rstd[:, g:g + 1],
                                                   ALU.subtract, ALU.mult)
                return last

            def over_experts(column):
                return column.unsqueeze(2).to_broadcast([P, G, E])

            def below_maximum(n):
                dve.wait_ge(gate_done, n + 1)
                nc.vector.tensor_tensor(logits[:], ps_s[:, 0:G * E].rearrange("p (g e) -> p g e", e=E),
                                        gate_b_rows[:].unsqueeze(1).to_broadcast([P, G, E]),
                                        ALU.add).then_inc(below_step, 1)
                dve.wait_ge(below_step, BELOW * n + 1)
                nc.vector.tensor_reduce(top_logit[:], logits[:], AX.X, ALU.max).then_inc(below_step, 1)
                dve.wait_ge(below_step, BELOW * n + 2)
                nc.vector.tensor_tensor(below_top[:], logits[:], over_experts(top_logit[:]),
                                        ALU.subtract).then_inc(below_step, 1)

            def first_choice(n):
                at = CHOICE * n
                nc.vector.scalar_tensor_tensor(keys[:, 0], below_top[:], 0.0, rank[:], ALU.is_ge, ALU.mult)\
                  .then_inc(choice_step, 1)
                dve.wait_ge(choice_step, at + 1)
                nc.vector.tensor_reduce(key[:, 0], keys[:, 0], AX.X, ALU.max).then_inc(choice_step, 1)
                dve.wait_ge(choice_step, at + 2)
                nc.vector.tensor_tensor(chosen[:, 0], keys[:, 0], over_experts(key[:, 0]), ALU.is_equal)\
                  .then_inc(choice_step, 1)
                dve.wait_ge(choice_step, at + 3)
                nc.vector.scalar_tensor_tensor(rest[:], chosen[:, 0], -3e38, below_top[:], ALU.mult, ALU.add)\
                  .then_inc(choice_step, 1)
                dve.wait_ge(choice_step, at + 4)
                nc.vector.tensor_reduce(best_rest[:], rest[:], AX.X, ALU.max).then_inc(choice_step, 1)

            def second_choice(n):
                at = CHOICE * n
                dve.wait_ge(choice_step, at + 5)
                nc.vector.tensor_tensor(below_best[:], rest[:], over_experts(best_rest[:]), ALU.subtract)\
                  .then_inc(choice_step, 1)
                dve.wait_ge(choice_step, at + 6)
                nc.vector.scalar_tensor_tensor(keys[:, 1], below_best[:], 0.0, rank[:], ALU.is_ge, ALU.mult)\
                  .then_inc(choice_step, 1)
                dve.wait_ge(choice_step, at + 7)
                nc.vector.tensor_reduce(key[:, 1], keys[:, 1], AX.X, ALU.max).then_inc(choice_step, 1)
                dve.wait_ge(choice_step, at + 8)
                nc.vector.tensor_tensor(chosen[:, 1], keys[:, 1], over_experts(key[:, 1]), ALU.is_equal)\
                  .then_inc(choice_step, 1)
                dve.wait_ge(choice_step, at + 9)
                nc.vector.tensor_tensor(both[:], chosen[:, 0], chosen[:, 1], ALU.add).then_inc(choice_step, 1)

            def combine_weights(n):
                dve.wait_ge(powers_ready, n + 1)
                nc.vector.tensor_reduce(total[:], powers[:], AX.X, ALU.add).then_inc(route_step, 1)
                dve.wait_ge(choice_step, CHOICE * (n + 1))
                nc.vector.tensor_tensor(kept[:], both[:], powers[:], ALU.mult).then_inc(route_step, 1)
                dve.wait_ge(route_step, ROUTE * n + 1)
                nc.vector.reciprocal(inv_total[:], total[:]).then_inc(route_step, 1)
                dve.wait_ge(route_step, ROUTE * n + 3)
                wait(dve, cw_t_done, n)
                nc.vector.tensor_tensor(cw[:], kept[:], over_experts(inv_total[:]), ALU.mult).then_inc(route_step, 1)

            def graph_output(n, j):
                dve.wait_ge(agg_done, n + 1)
                deg = ps_gnn[:, :, P]
                nc.vector.tensor_scalar(deg_max[:], deg, 1.0, None, ALU.max).then_inc(deg_step, 1)
                nc.vector.tensor_scalar(deg_pos[:], deg, 0.0, None, ALU.is_gt).then_inc(deg_step, 1)
                dve.wait_ge(deg_step, DEG * n + 1)
                nc.vector.reciprocal(deg_inv[:], deg_max[:]).then_inc(deg_step, 1)
                dve.wait_ge(deg_step, DEG * n + 3)
                nc.vector.tensor_tensor(deg_scale[:], deg_inv[:], deg_pos[:], ALU.mult).then_inc(deg_step, 1)
                dve.wait_ge(deg_step, DEG * n + 4)
                for g in range(G):
                    last = nc.vector.scalar_tensor_tensor(pre_relu[:, g], ps_gnn[:, g, 0:P], deg_scale[:, g:g + 1],
                                                          upd_bias[:, g], ALU.mult, ALU.add)
                last.then_inc(pre_relu_ready, 1)
                dve.wait_ge(pre_relu_ready, n + 1)
                nc.vector.scalar_tensor_tensor(x2[:, j], pre_relu[:], 0.0, xs[:, j], ALU.max, ALU.add)\
                  .then_inc(x2_ready, 1)

            def weigh(n, j, e):
                if e == 0:
                    dve.wait_ge(cw_in[j % 2], 16 * (n // 2 + 1) if isinstance(n, int) else 8 * (n - j % 2) + 16)
                    wait(dve, result_t_done, n - 1)
                    to = acc[:, j % 2]
                else:
                    wait(dve, added, (E - 1) * n + e - (4 if e > 4 else 7 if e == 4 else 3))
                    to = weighted[:, e % 4]
                dve.wait_ge(y_done, E * n + e + 1)
                nc.vector.scalar_tensor_tensor(to, ps_y[:, e % 2], b2_cols[:, e:e + 1], cw_rows[:, j % 2, e],
                                               ALU.add, ALU.mult).then_inc(y_used, 1)

            def tile(i, j):
                j2, j3 = (j + 2) % SLOTS, (j + 3) % SLOTS
                for s in range(E):
                    if s == 0 and inside(i + 3):
                        m = i + 3
                        dve.wait_ge(x_in[j3], 16 * (m // SLOTS + 1) if isinstance(m, int) else 4 * (m - j3) + 16)
                        statistics(m, xs[:, j3], stats1_step, stats1, mean1, var1)
                    if s == 1 and inside(i + 1):
                        below_maximum(i + 1)
                    if s == 1 and inside(i + 2):
                        dve.wait_ge(msg_ready, i + 3)
                        nc.vector.tensor_tensor(upd_bias[:], ps_gnn[:, :, P:],
                                                bias_rows[:].unsqueeze(1).to_broadcast([P, G, P]),
                                                ALU.add).then_inc(upd_ready, 1)
                    if s == 2 and inside(i + 1):
                        dve.wait_ge(below_step, BELOW * (i + 2))
                        first_choice(i + 1)
                    if s == 3 and inside(i + 2):
                        graph_output(i + 2, j2)
                    if s == 3 and inside(i + 1):
                        second_choice(i + 1)
                    if s == 4 and inside(i + 2):
                        dve.wait_ge(x2_ready, i + 3)
                        statistics(i + 2, x2[:, j2], stats2_step, stats2, mean2, var2)
                    if s == 4 and inside(i + 1):
                        combine_weights(i + 1)
                    if s == 5 and inside(i + 2):
                        dve.wait_ge(rstd2_ready, i + 3)
                        wait(dve, xn2_t_done, i + 2)
                        normalise(x2[:, j2], mean2, rstd2, xn2).then_inc(xn2_ready, 1)
                    if s == 5 and inside(i - 1):
                        m, q = i - 1, (j - 1) % SLOTS
                        dve.wait_ge(result_t_done, m + 1)
                        wait(dve, out_stored[q % 2], 16 * (m // 2) if isinstance(m, int) else 8 * (m - q % 2))
                        nc.vector.tensor_tensor(result[:, q % 2], ps_t[:], x2[:, q], ALU.add).then_inc(result_ready, 1)
                    if s == 6 and inside(i + 3):
                        dve.wait_ge(rstd1_ready, i + 4)
                        wait(dve, xn1_t_done, i + 3)
                        normalise(xs[:, j3], mean1, rstd1, xn1).then_inc(xn1_ready, 1)
                    if s == 7 and inside(i + 2):
                        dve.wait_ge(xt_hi_ready, i + 3)
                        nc.vector.tensor_tensor(xt_lo[:, j2], ps_t[:].rearrange("p g t -> p (g t)"),
                                                xt_hi[:, j2].bitcast(F32), ALU.subtract).then_inc(xt_ready, 1)
                    e = (s - LAG) % E
                    n, k = (i, j) if s >= LAG else (i - 1, (j - 1) % SLOTS)
                    if inside(n):
                        weigh(n, k, e)
                    if inside(i):
                        ex = E * i + s
                        dve.wait_ge(gel_hi_ready, ex + 1)
                        nc.vector.tensor_tensor(gel_lo[:, s % 4], gel[:, s % 2], gel_hi[:, s % 4].bitcast(F32),
                                                ALU.subtract).then_inc(gel_ready, 1)
                if isinstance(i, int) and i == -2:
                    split_weights()

            dve.wait_ge(consts_in, 7 * 16)
            dve.wait_ge(consts_ready, 1)
            every_tile(dve, tile)

        @block.tensor
        def _(pe):
            pe.wait_ge(consts_in, 7 * 16)
            pe.wait_ge(consts_ready, 1)

            def first_product(n, j, e):
                ex = E * n + e
                for c in range(HC):
                    wait(pe, gel_done, HC * (ex - 1) + c + 1)
                    cols = slice(c * P, c * P + P)
                    nc.tensor.matmul(ps_hid[:, c], w1_hi[:, e, cols], xt_hi[:, j], start=True, stop=False)
                    nc.tensor.matmul(ps_hid[:, c], w1_hi[:, e, cols], xt_lo[:, j], start=False, stop=False)
                    nc.tensor.matmul(ps_hid[:, c], w1_lo[:, e, cols], xt_hi[:, j], start=False, stop=True)\
                      .then_inc(hid_done, 1)

            def second_product(n, e):
                ex = E * n + e
                pe.wait_ge(gel_ready, ex + 1)
                wait(pe, y_used, ex - 1)
                for c in range(HC):
                    w = HC * e + c
                    nc.tensor.matmul(ps_y[:, e % 2], w2_hi[:, w], gel_hi[:, e % 4, c], start=c == 0, stop=False)
                    nc.tensor.matmul(ps_y[:, e % 2], w2_hi[:, w], gel_lo[:, e % 4, c], start=False, stop=False)
                    last = nc.tensor.matmul(ps_y[:, e % 2], w2_lo[:, w], gel_hi[:, e % 4, c],
                                            start=False, stop=c == HC - 1)
                last.then_inc(y_done, 1)

            def tile(i, j):
                j2 = (j + 2) % SLOTS
                if isinstance(i, int) and i == 0:
                    pe.wait_ge(w_ready, 3)
                for s in range(E):
                    if s == 0 and inside(i + 2):
                        n = i + 2
                        pe.wait_ge(xn1_t_ready, n + 1)
                        for g in range(G):
                            last = nc.tensor.matmul(ps_gnn[:, g], xn1_t[:, g], w_gnn[:], start=True, stop=True)
                        last.then_inc(gnn_done, 1)
                    if s == 0 and inside(i + 1):
                        n, k = i + 1, (j + 1) % SLOTS
                        pe.wait_ge(xt_ready, n + 1)
                        pe.wait_ge(w_ready, 1)
                        wait(pe, cw_t_ready, n)
                        for g in range(G):
                            at = slice(g * P, g * P + P)
                            to = ps_s[:, g * E:g * E + E]
                            nc.tensor.matmul(to, xt_hi[:, k, at], gate_hi[:], start=True, stop=False)
                            nc.tensor.matmul(to, xt_lo[:, k, at], gate_hi[:], start=False, stop=False)
                            last = nc.tensor.matmul(to, xt_hi[:, k, at], gate_lo[:], start=False, stop=True)
                        last.then_inc(gate_done, 1)
                    if s == 2 and inside(i + 2):
                        n = i + 2
                        pe.wait_ge(adj_in[j2], 16 * (n // SLOTS + 1) if isinstance(n, int) else 4 * (n - j2) + 16)
                        pe.wait_ge(upd_ready, n + 1)
                        for g in range(G):
                            last = nc.tensor.matmul(ps_gnn[:, g, 0:P + 1], adjs[:, j2, g], msg_rows[:, g],
                                                    start=True, stop=True)
                        last.then_inc(agg_done, 1)
                    if s == 4 and inside(i - 1):
                        n, k = i - 1, (j - 1) % 2
                        pe.wait_ge(added, (E - 1) * (n + 1))
                        pe.wait_ge(xt_ready, at_most(n + 3, TILES))
                        wait(pe, result_ready, n)
                        for g in range(G):
                            last = nc.tensor.transpose(ps_t[:, g], acc[:, k, g * P:g * P + P], ident[:])
                        last.then_inc(result_t_done, 1)
                    if s == 5 and inside(i + 1):
                        n = i + 1
                        pe.wait_ge(route_step, ROUTE * (n + 1))
                        for g in range(G):
                            last = nc.tensor.transpose(ps_s[0:E, g * P:g * P + P], cw[:, g], ident[:])
                        last.then_inc(cw_t_done, 1)
                    if s == 6 and inside(i + 2):
                        n = i + 2
                        pe.wait_ge(xn2_ready, n + 1)
                        wait(pe, result_ready, i)
                        for g in range(G):
                            last = nc.tensor.transpose(ps_t[:, g], xn2[:, g], ident[:])
                        last.then_inc(xn2_t_done, 1)
                    if s == 7 and inside(i + 3):
                        n = i + 3
                        pe.wait_ge(xn1_ready, n + 1)
                        wait(pe, pre_relu_ready, n)
                        for g in range(G):
                            last = nc.tensor.transpose(xn1_ps[:, g], xn1[:, g], ident[:])
                        last.then_inc(xn1_t_done, 1)
                    if inside(i):
                        first_product(i, j, s)
                    e = (s - LAG) % E
                    n = i if s >= LAG else i - 1
                    if inside(n):
                        second_product(n, e)

            every_tile(pe, tile)


_INS = ["x", "adj", "L0_gnn_W_msg", "L0_gnn_W_upd", "L0_gnn_bias", "L0_ffn_gate_w", "L0_ffn_gate_b",
        "L0_ffn_W1", "L0_ffn_b1", "L0_ffn_W2", "L0_ffn_b2"]


def kernel(**inputs):
    import numpy as np
    import concourse.bacc as bacc
    from concourse.bass_utils import run_bass_kernel_spmd as run

    nc = bacc.Bacc("TRN2", target_bir_lowering=False, num_devices=1)
    arrays, args = {}, []
    for name in _INS:
        a = np.ascontiguousarray(inputs[name])
        arrays[f"in_{name}"] = a
        args.append(nc.dram_tensor(f"in_{name}", a.shape, mybir.dt.from_np(a.dtype), kind="ExternalInput").ap())
    out = nc.dram_tensor("out", (GRAPHS, P, P), F32, kind="ExternalOutput").ap()
    cw_dram = nc.dram_tensor("cw_dram", (TILES, E, TOK), F32, kind="Internal").ap()
    gnn_moe(nc, *args, out, cw_dram)
    return run(nc, [arrays], core_ids=[0]).results[0]["out"]
```

```python
from contextlib import ExitStack

import concourse.bass as bass
from concourse import mybir

F32 = mybir.dt.float32
F32R = mybir.dt.float32r
ACT = mybir.ActivationFunctionType
ALU = mybir.AluOpType
AX = mybir.AxisListType

P = 128
GRAPHS = 128
G = 4
TOK = G * P
TILES = GRAPHS // G
E = 8
H = 256
HC = H // P
EPS = 1e-5
SLOTS = 4
LAG = 3



def wait(engine, sem, count):
    if not isinstance(count, int) or count > 0:
        engine.wait_ge(sem, count)


def inside(n):
    return not isinstance(n, int) or 0 <= n < TILES


def at_most(n, most):
    return min(n, most) if isinstance(n, int) else n


def first_half(i, s):
    if isinstance(i, int) and i == -1 and s >= E - LAG:
        return 0, s - (E - LAG)
    if not inside(i) or isinstance(i, int) and i == 0 and s < LAG:
        return None
    return i, s


def finished(i):
    if not isinstance(i, int):
        return [2]
    return [back for back in ([2, 1] if i == TILES else [2]) if i - back >= 0]


def every_tile(engine, tile):
    for i in range(-4, SLOTS):
        tile(i, i % SLOTS)
    with engine.Fori(SLOTS, TILES - 2 * SLOTS + 1, SLOTS) as first:
        for j in range(SLOTS):
            tile(first + j, j)
    for i in range(TILES - SLOTS, TILES + 1):
        tile(i, i % SLOTS)


def gnn_moe(nc, x, adj, w_msg, w_upd, gnn_bias, gate_w, gate_b, w1, b1, w2, b2, out, cw_dram):
    x_t = x.rearrange("(t g) n f -> t n g f", g=G)
    adj_t = adj.rearrange("(t g) i j -> t i g j", g=G)
    out_t = out.rearrange("(t g) n f -> t n g f", g=G)

    ctx = ExitStack()
    with ctx:
        def sb(name, shape, dt=F32):
            return ctx.enter_context(nc.sbuf_tensor(name, shape, dt))

        def pb(name, shape):
            return ctx.enter_context(nc.psum_tensor(name, shape, F32))

        def sem(name):
            return ctx.enter_context(nc.semaphore(name))

        w1_raw = sb("w1_raw", [P, E, H])
        w2_raw = sb("w2_raw", [P, E * HC, P])
        w1_hi = sb("w1_hi", [P, E, H], F32R)
        w1_lo = sb("w1_lo", [P, E, H], F32R)
        w2_hi = sb("w2_hi", [P, E * HC, P], F32R)
        w2_lo = sb("w2_lo", [P, E * HC, P], F32R)
        w_gnn = sb("w_gnn", [P, 2 * P])
        w_gnn_hi = sb("w_gnn_hi", [P, 2 * P], F32R)
        w_gnn_lo = sb("w_gnn_lo", [P, 2 * P], F32R)
        bias_rows = sb("bias_rows", [P, P])
        gate_raw = sb("gate_raw", [P, E])
        gate_split = sb("gate_split", [P, 2, E], F32R)
        gate_b_rows = sb("gate_b_rows", [P, E])
        b1_cols = sb("b1_cols", [P, E * HC])
        b2_cols = sb("b2_cols", [P, E])
        ident = sb("ident", [P, P])
        euler = sb("euler", [P, G, E])
        neg_half = sb("neg_half", [P, G])
        rank = sb("rank", [P, G, E])

        xs = sb("xs", [P, SLOTS, G, P])
        adjs = sb("adjs", [P, SLOTS, G, P])
        stats1 = sb("stats1", [P, G, 6])
        neg_mean1 = sb("neg_mean1", [P, G])
        var1 = sb("var1", [P, G])
        rstd1 = sb("rstd1", [P, G])
        shift1 = sb("shift1", [P, G])
        xn1 = sb("xn1", [P, G, P])
        xn1_hi = sb("xn1_hi", [P, G, P], F32R)
        xn1_lo = sb("xn1_lo", [P, G, P], F32R)
        msg_rows = sb("msg_rows", [P, G, P + 1])
        upd_rows = sb("upd_rows", [P, G, P])
        upd_bias = sb("upd_bias", [P, G, P])
        deg_max = sb("deg_max", [P, G])
        deg_pos = sb("deg_pos", [P, G])
        deg_inv = sb("deg_inv", [P, G])
        deg_scale = sb("deg_scale", [P, G])
        pre_relu = sb("pre_relu", [P, G, P])
        x2 = sb("x2", [P, SLOTS, G, P])
        stats2 = sb("stats2", [P, G, 6])
        neg_mean2 = sb("neg_mean2", [P, G])
        var2 = sb("var2", [P, G])
        rstd2 = sb("rstd2", [P, G])
        xn2 = sb("xn2", [P, G, P])
        xt_hi = sb("xt_hi", [P, SLOTS, TOK], F32R)
        xt_lo = sb("xt_lo", [P, SLOTS, TOK], F32R)

        mean_gap = sb("mean_gap", [P, G])
        mean_sum = sb("mean_sum", [P, G])
        sq_sum = sb("sq_sum", [P, G])
        gap_sq = sb("gap_sq", [P, G])
        sq_all = sb("sq_all", [P, G])

        upper_logits = sb("upper_logits", [P, G, E])
        logits = sb("logits", [P, G, E])
        top_logit = sb("top_logit", [P, G])
        below_top = sb("below_top", [P, G, E])
        powers = sb("powers", [P, G, E])
        total = sb("total", [P, G])
        inv_total = sb("inv_total", [P, G])
        keys = sb("keys", [P, 2, G, E])
        key = sb("key", [P, 2, G])
        chosen = sb("chosen", [P, 2, G, E])
        rest = sb("rest", [P, G, E])
        best_rest = sb("best_rest", [P, G])
        below_best = sb("below_best", [P, G, E])
        both = sb("both", [P, G, E])
        kept = sb("kept", [P, G, E])
        cw = sb("cw", [P, G, E])
        cw_t = sb("cw_t", [G * E, 2, P])
        cw_rows = sb("cw_rows", [P, 2, G, E, P])

        gel = sb("gel", [P, 2, HC, TOK])
        gel_hi = sb("gel_hi", [P, 4, HC, TOK], F32R)
        gel_lo = sb("gel_lo", [P, 4, HC, TOK], F32R)
        weighted = sb("weighted", [P, 4, TOK])
        acc = sb("acc", [P, 2, TOK])
        result = sb("result", [P, 2, G, P])

        ps_hid = pb("ps_hid", [P, HC, TOK])
        ps_y = pb("ps_y", [P, 2, TOK])
        ps_gnn = pb("ps_gnn", [P, G, 2 * P])
        ps_t = pb("ps_t", [P, G, P])
        ps_s = pb("ps_s", [P, TOK])

        xn1_ps = ps_gnn[:, 0:2].rearrange("p a (g t) -> p (a g) t", g=2)

        gate_ps = ps_s[:, 0:G * 2 * E].rearrange("p (g h e) -> p g h e", h=2, e=E)

        gnn_in = sem("gnn_in")
        gate_in = sem("gate_in")
        biases_in = sem("biases_in")
        w_in = sem("w_in")
        w_hi_ready = sem("w_hi_ready")
        w_ready = sem("w_ready")
        w2_lo_ready = sem("w2_lo_ready")
        blank = sem("blank")
        consts_ready = sem("consts_ready")
        x_in = [sem(f"x_in{j}") for j in range(SLOTS)]
        adj_in = [sem(f"adj_in{j}") for j in range(SLOTS)]
        stats1_step = sem("stats1_step")
        rstd1_ready = sem("rstd1_ready")
        shift1_ready = sem("shift1_ready")
        xn1_ready = sem("xn1_ready")
        xn1_t_done = sem("xn1_t_done")
        xn1_hi_ready = sem("xn1_hi_ready")
        xn1_t_ready = sem("xn1_t_ready")
        gnn_done = sem("gnn_done")
        msg_ready = sem("msg_ready")
        upd_ready = sem("upd_ready")
        upd_bias_ready = sem("upd_bias_ready")
        agg_done = sem("agg_done")
        deg_step = sem("deg_step")
        pre_relu_ready = sem("pre_relu_ready")
        x2_ready = sem("x2_ready")
        stats2_step = sem("stats2_step")
        rstd2_ready = sem("rstd2_ready")
        xn2_ready = sem("xn2_ready")
        xn2_t_done = sem("xn2_t_done")
        xt_hi_ready = sem("xt_hi_ready")
        xt_ready = sem("xt_ready")
        gate_done = sem("gate_done")
        below_step = sem("below_step")
        choice_step = sem("choice_step")
        powers_ready = sem("powers_ready")
        route_step = sem("route_step")
        cw_t_done = sem("cw_t_done")
        cw_t_ready = sem("cw_t_ready")
        cw_stored = [sem(f"cw_stored{j}") for j in range(2)]
        cw_in = [[sem(f"cw_in{j}_{half}") for half in range(2)] for j in range(2)]
        hid_done = sem("hid_done")
        gel_done = sem("gel_done")
        gel_hi_ready = sem("gel_hi_ready")
        gel_ready = sem("gel_ready")
        y_done = sem("y_done")
        y_used = sem("y_used")
        added = sem("added")
        result_t_done = sem("result_t_done")
        result_ready = sem("result_ready")
        out_stored = [sem(f"out_stored{j}") for j in range(2)]

        STATS = 8
        DEG = 4
        BELOW = 4
        CHOICE = 10
        ROUTE = 4

        block = ctx.enter_context(nc.Block())

        @block.sync
        def _(sp):
            def load_x(n, j):
                wait(sp, x2_ready, n - SLOTS + 1)
                sp.dma_start(xs[:, j], x_t[n]).then_inc(x_in[j], 16)

            load_x(0, 0)
            sp.dma_start(w_gnn[:, 0:P], w_msg).then_inc(gnn_in, 16)
            sp.dma_start(w_gnn[:, P:], w_upd).then_inc(gnn_in, 16)
            sp.dma_start(bias_rows[:], gnn_bias.partition_broadcast(P)).then_inc(gnn_in, 16)
            sp.dma_start(gate_raw[:], gate_w).then_inc(gate_in, 16)
            sp.dma_start(gate_b_rows[:], gate_b.partition_broadcast(P)).then_inc(gate_in, 16)
            load_x(1, 1)
            sp.dma_start(w1_raw[:], w1.rearrange("e d h -> d e h")).then_inc(w_in, 16)
            sp.dma_start(w2_raw[:], w2.rearrange("e (c h) d -> h (e c) d", c=HC)).then_inc(w_in, 16)
            load_x(2, 2)
            with nc.allow_non_contiguous_dma(reason="12 KB of biases, once"):
                sp.dma_start(b1_cols[:], b1.rearrange("e (c h) -> h (e c)", c=HC)).then_inc(biases_in, 16)
                sp.dma_start(b2_cols[:], b2.rearrange("e d -> d e")).then_inc(biases_in, 16)
            load_x(3, 3)

            def tile(i, j):
                if inside(i) and inside(i + SLOTS):
                    load_x(i + SLOTS, j)
                for back in finished(i):
                    n, k = i - back, (j - back) % 2
                    sp.wait_ge(result_ready, n + 1)
                    sp.dma_start(out_t[n], result[:, k]).then_inc(out_stored[k], 16)
                if inside(i + 1):
                    n, k = i + 1, (j + 1) % 2
                    sp.compute_val(n + 1)
                    sp.compute_val(E * (n - 1))
                    sp.wait_ge(cw_t_ready, n + 1)
                    sp.dma_start(cw_dram[n], cw_t[:, k]).then_inc(cw_stored[k], 16)
                    sp.wait_ge(cw_stored[k], 16 * (n // 2 + 1) if isinstance(n, int) else 8 * (n - k) + 16)
                    wait(sp, y_used, E * (n - 1))
                    for half in range(2):
                        at = slice(half * E // 2, (half + 1) * E // 2)
                        sp.dma_start(cw_rows[:, k, :, at],
                                     cw_dram[n].rearrange("(g e) t -> g e t", e=E)[:, at].partition_broadcast(P))\
                          .then_inc(cw_in[k][half], 16)

            every_tile(sp, tile)
            for k in range(2):
                sp.wait_ge(out_stored[k], 16 * (TILES // 2))

        @block.gpsimd
        def _(pool):
            def load_adj(n, j):
                wait(pool, agg_done, n - SLOTS + 1)
                pool.dma_start(adjs[:, j], adj_t[n]).then_inc(adj_in[j], 16)

            for j in range(2):
                load_adj(j, j)
            nc.gpsimd.memset(neg_half[:], -0.5)
            nc.gpsimd.memset(ident[:], 0.0).then_inc(blank, 1)
            nc.gpsimd.memset(msg_rows[:, :, P:], 1.0)
            nc.gpsimd.memset(euler[:], 2.718281828459045)
            for e in range(E):
                nc.gpsimd.memset(rank[:, :, e:e + 1], float(E - e))
            pool.wait_ge(blank, 1)
            nc.gpsimd.affine_select(out=ident[:], in_=ident[:], compare_op=ALU.not_equal, fill=1.0, base=0,
                                    pattern=[[-1, P]], channel_multiplier=1).then_inc(consts_ready, 1)
            pool.wait_ge(consts_ready, 1)

            def inverse_deviation(n, stats_step, var, ready, rstd):
                pool.wait_ge(stats_step, STATS * (n + 1))
                nc.gpsimd.tensor_tensor(rstd[:], var[:], neg_half[:], ALU.pow).then_inc(ready, 1)

            def add(n, j, e):
                pool.wait_ge(y_used, E * n + e + 1)
                if e > 1:
                    pool.wait_ge(added, (E - 1) * n + e - 1)
                nc.gpsimd.tensor_tensor(acc[:, j % 2], acc[:, j % 2], weighted[:, e % 4], ALU.add).then_inc(added, 1)

            def half_of_powers(n, half):
                pool.wait_ge(below_step, BELOW * (n + 1))
                wait(pool, route_step, ROUTE * n)
                at = slice(half * G // 2, (half + 1) * G // 2)
                nc.gpsimd.tensor_tensor(powers[:, at], euler[:, at], below_top[:, at], ALU.pow).then_inc(powers_ready, 1)

            def lower_second_weights():
                pool.wait_ge(w_hi_ready, 4)
                pool.wait_ge(w_in, 2 * 16)
                nc.gpsimd.tensor_tensor(w2_lo[:], w2_raw[:], w2_hi[:].bitcast(F32), ALU.subtract).then_inc(w2_lo_ready, 1)

            def update_bias(n):
                pool.wait_ge(upd_ready, n + 1)
                wait(pool, pre_relu_ready, n)
                nc.gpsimd.tensor_tensor(upd_bias[:], upd_rows[:], bias_rows[:].unsqueeze(1).to_broadcast([P, G, P]),
                                        ALU.add).then_inc(upd_bias_ready, 1)

            def tile(i, j):
                ahead = isinstance(i, int) and i < 0
                first = isinstance(i, int) and i == -3
                if first:
                    for slot in range(2, SLOTS):
                        load_adj(slot, slot)
                if isinstance(i, int) and i == -2:
                    lower_second_weights()
                for s in range(E):
                    if s == 5 and inside(i) and inside(i + SLOTS):
                        load_adj(i + SLOTS, j)
                    if s == (2 if ahead else 4) and inside(i + 2):
                        inverse_deviation(i + 2, stats2_step, var2, rstd2_ready, rstd2)
                    if s == 7 and inside(i + 3) and not first:
                        update_bias(i + 3)
                    e = (s - LAG) % E
                    n, k = (i, j) if s >= LAG else (i - 1, j - 1)
                    if inside(n) and e > 0:
                        add(n, k, e)
                    if s in (1, 2) and inside(i + 1):
                        half_of_powers(i + 1, s - 1)
                    if s == 7 and inside(i + 4):
                        wait(pool, xn1_ready, G * (i + 4))
                        inverse_deviation(i + 4, stats1_step, var1, rstd1_ready, rstd1)
                        pool.wait_ge(rstd1_ready, i + 5)
                        nc.gpsimd.tensor_tensor(shift1[:], neg_mean1[:], rstd1[:], ALU.mult).then_inc(shift1_ready, 1)
                    if s == 7 and first:
                        pool.wait_ge(gnn_in, 3 * 16)
                        update_bias(0)

            every_tile(pool, tile)

        @block.scalar
        def _(act):
            act.wait_ge(gnn_in, 3 * 16)
            nc.scalar.activation(w_gnn_hi[:], w_gnn[:], ACT.Copy).then_inc(w_hi_ready, 1)

            def upper_weights():
                act.wait_ge(gate_in, 2 * 16)
                nc.scalar.activation(gate_split[:, 0], gate_raw[:], ACT.Copy).then_inc(w_hi_ready, 1)
                act.wait_ge(w_in, 2 * 16)
                nc.scalar.activation(w1_hi[:], w1_raw[:], ACT.Copy).then_inc(w_hi_ready, 1)

            def upper_second_weights():
                nc.scalar.activation(w2_hi[:], w2_raw[:], ACT.Copy).then_inc(w_hi_ready, 1)
                act.wait_ge(biases_in, 2 * 16)

            def first_norm(slot, g):
                nc.scalar.activation(xn1[:, g], xs[:, slot, g], ACT.Identity, bias=shift1[:, g:g + 1],
                                     scale=rstd1[:, g:g + 1]).then_inc(xn1_ready, 1)

            def tile(i, j):
                for s in range(E):
                    if s == 7 and inside(i + 1):
                        n, k = i + 1, (j + 1) % 2
                        act.wait_ge(cw_t_done, n + 1)
                        wait(act, cw_stored[k], 16 * (n // 2) if isinstance(n, int) else 8 * (n - k))
                        nc.scalar.activation(cw_t[:, k], ps_s[0:G * E, 0:P], ACT.Copy).then_inc(cw_t_ready, 1)
                    if first_half(i, s):
                        n, e = first_half(i, s)
                        ex = E * n + e
                        wait(act, gel_ready, ex - 1)
                        for c in range(HC):
                            act.wait_ge(hid_done, HC * ex + c + 1)
                            nc.scalar.activation(gel[:, e % 2, c], ps_hid[:, c], ACT.Gelu,
                                                 bias=b1_cols[:, HC * e + c:HC * e + c + 1]).then_inc(gel_done, 1)
                        act.wait_ge(gel_done, HC * ex + HC)
                        wait(act, y_done, ex - 3)
                        nc.scalar.activation(gel_hi[:, e % 4], gel[:, e % 2], ACT.Copy).then_inc(gel_hi_ready, 1)
                    if s < G and inside(i + 3):
                        if s == 0:
                            act.wait_ge(shift1_ready, i + 4)
                            wait(act, xn1_t_done, i + 3)
                        first_norm((j + 3) % SLOTS, s)
                    if s == 4 and inside(i + 3):
                        n = i + 3
                        act.wait_ge(xn1_t_done, n + 1)
                        wait(act, gnn_done, n)
                        nc.scalar.activation(xn1_hi[:], xn1_ps, ACT.Copy).then_inc(xn1_hi_ready, 1)
                        if isinstance(i, int) and i == -3:
                            upper_weights()
                    if s == 6 and inside(i + 3):
                        n = i + 3
                        act.wait_ge(gnn_done, n + 1)
                        wait(act, agg_done, n)
                        nc.scalar.activation(msg_rows[:, :, 0:P], ps_gnn[:, :, 0:P], ACT.Copy).then_inc(msg_ready, 1)
                        wait(act, upd_bias_ready, n)
                        nc.scalar.activation(upd_rows[:], ps_gnn[:, :, P:], ACT.Copy).then_inc(upd_ready, 1)
                        if isinstance(i, int) and i == -3:
                            upper_second_weights()
                    if s == 6 and inside(i + 2):
                        act.wait_ge(xn2_t_done, i + 3)
                        nc.scalar.activation(xt_hi[:, (j + 2) % SLOTS], ps_t[:].rearrange("p g t -> p (g t)"),
                                             ACT.Copy).then_inc(xt_hi_ready, 1)

            every_tile(act, tile)

        @block.vector
        def _(dve):
            def lower_graph_weights():
                dve.wait_ge(w_hi_ready, 1)
                dve.wait_ge(gnn_in, 3 * 16)
                nc.vector.tensor_tensor(w_gnn_lo[:], w_gnn[:], w_gnn_hi[:].bitcast(F32), ALU.subtract).then_inc(w_ready, 1)

            def lower_weights():
                dve.wait_ge(w_hi_ready, 2)
                dve.wait_ge(gate_in, 2 * 16)
                nc.vector.tensor_tensor(gate_split[:, 1], gate_raw[:], gate_split[:, 0].bitcast(F32),
                                        ALU.subtract).then_inc(w_ready, 1)
                dve.wait_ge(w_hi_ready, 3)
                dve.wait_ge(w_in, 2 * 16)
                nc.vector.tensor_tensor(w1_lo[:], w1_raw[:], w1_hi[:].bitcast(F32), ALU.subtract).then_inc(w_ready, 1)
                dve.wait_ge(biases_in, 2 * 16)
                dve.wait_ge(consts_ready, 1)

            def row_statistics(rows, step, stats):
                for g in range(G):
                    last = nc.vector.bn_stats(stats[:, g], rows[:, g])
                last.then_inc(step, 1)

            def means(n, step, stats, neg_mean):
                mean_e, mean_o, sq_e, sq_o = stats[:, :, 1], stats[:, :, 4], stats[:, :, 2], stats[:, :, 5]
                dve.wait_ge(step, STATS * n + 1)
                nc.vector.tensor_tensor(mean_gap[:], mean_e, mean_o, ALU.subtract).then_inc(step, 1)
                nc.vector.tensor_tensor(mean_sum[:], mean_e, mean_o, ALU.add).then_inc(step, 1)
                nc.vector.tensor_tensor(sq_sum[:], sq_e, sq_o, ALU.add).then_inc(step, 1)
                dve.wait_ge(step, STATS * n + 2)
                nc.vector.scalar_tensor_tensor(gap_sq[:], mean_gap[:], P / 4.0, mean_gap[:], ALU.mult, ALU.mult)\
                  .then_inc(step, 1)
                dve.wait_ge(step, STATS * n + 3)
                nc.vector.tensor_scalar(neg_mean[:], mean_sum[:], -0.5, None, ALU.mult).then_inc(step, 1)

            def squares(n, step):
                dve.wait_ge(step, STATS * n + 5)
                nc.vector.tensor_tensor(sq_all[:], sq_sum[:], gap_sq[:], ALU.add).then_inc(step, 1)

            def variances(n, step, var):
                dve.wait_ge(step, STATS * n + 7)
                nc.vector.tensor_scalar(var[:], sq_all[:], 1.0 / P, EPS, ALU.mult, ALU.add).then_inc(step, 1)

            def normalise(rows, neg_mean, rstd, normed):
                for g in range(G):
                    last = nc.vector.tensor_scalar(normed[:, g], rows[:, g], neg_mean[:, g:g + 1], rstd[:, g:g + 1],
                                                   ALU.add, ALU.mult)
                return last

            def lower_first_norm(n):
                dve.wait_ge(xn1_hi_ready, n + 1)
                wait(dve, gnn_done, n)
                nc.vector.tensor_tensor(xn1_lo[:], xn1_ps, xn1_hi[:].bitcast(F32), ALU.subtract)\
                  .then_inc(xn1_t_ready, 1)

            def over_experts(column):
                return column.unsqueeze(2).to_broadcast([P, G, E])

            def biased_logits(n):
                dve.wait_ge(gate_done, n + 1)
                nc.vector.tensor_tensor(upper_logits[:], gate_ps[:, :, 0],
                                        gate_b_rows[:].unsqueeze(1).to_broadcast([P, G, E]),
                                        ALU.add).then_inc(below_step, 1)

            def whole_logits(n):
                dve.wait_ge(below_step, BELOW * n + 1)
                nc.vector.tensor_tensor(logits[:], gate_ps[:, :, 1], upper_logits[:], ALU.add).then_inc(below_step, 1)

            def maximum(n):
                dve.wait_ge(below_step, BELOW * n + 2)
                nc.vector.tensor_reduce(top_logit[:], logits[:], AX.X, ALU.max).then_inc(below_step, 1)

            def below_maximum(n):
                dve.wait_ge(below_step, BELOW * n + 3)
                nc.vector.tensor_tensor(below_top[:], logits[:], over_experts(top_logit[:]),
                                        ALU.subtract).then_inc(below_step, 1)

            def first_keys(n):
                dve.wait_ge(below_step, BELOW * (n + 1))
                nc.vector.scalar_tensor_tensor(keys[:, 0], below_top[:], 0.0, rank[:], ALU.is_ge, ALU.mult)\
                  .then_inc(choice_step, 1)

            def second_keys(n):
                dve.wait_ge(choice_step, CHOICE * n + 6)
                nc.vector.scalar_tensor_tensor(keys[:, 1], below_best[:], 0.0, rank[:], ALU.is_ge, ALU.mult)\
                  .then_inc(choice_step, 1)

            def highest_key(n, k):
                dve.wait_ge(choice_step, CHOICE * n + (7 if k else 1))
                nc.vector.tensor_reduce(key[:, k], keys[:, k], AX.X, ALU.max).then_inc(choice_step, 1)

            def mark(n, k):
                dve.wait_ge(choice_step, CHOICE * n + (8 if k else 2))
                nc.vector.tensor_tensor(chosen[:, k], keys[:, k], over_experts(key[:, k]), ALU.is_equal)\
                  .then_inc(choice_step, 1)

            def leave_first(n):
                dve.wait_ge(choice_step, CHOICE * n + 3)
                nc.vector.scalar_tensor_tensor(rest[:], chosen[:, 0], -3e38, below_top[:], ALU.mult, ALU.add)\
                  .then_inc(choice_step, 1)

            def best_of_rest(n):
                dve.wait_ge(choice_step, CHOICE * n + 4)
                nc.vector.tensor_reduce(best_rest[:], rest[:], AX.X, ALU.max).then_inc(choice_step, 1)

            def below_best_of_rest(n):
                dve.wait_ge(choice_step, CHOICE * n + 5)
                nc.vector.tensor_tensor(below_best[:], rest[:], over_experts(best_rest[:]), ALU.subtract)\
                  .then_inc(choice_step, 1)

            def both_choices(n):
                dve.wait_ge(choice_step, CHOICE * n + 9)
                nc.vector.tensor_tensor(both[:], chosen[:, 0], chosen[:, 1], ALU.add).then_inc(choice_step, 1)

            def totals(n):
                dve.wait_ge(powers_ready, 2 * (n + 1))
                nc.vector.tensor_reduce(total[:], powers[:], AX.X, ALU.add).then_inc(route_step, 1)

            def keep_chosen(n):
                dve.wait_ge(choice_step, CHOICE * (n + 1))
                nc.vector.tensor_tensor(kept[:], both[:], powers[:], ALU.mult).then_inc(route_step, 1)

            def invert_totals(n):
                dve.wait_ge(route_step, ROUTE * n + 1)
                nc.vector.reciprocal(inv_total[:], total[:]).then_inc(route_step, 1)

            def combine_weights(n):
                dve.wait_ge(route_step, ROUTE * n + 3)
                wait(dve, cw_t_done, n)
                nc.vector.tensor_tensor(cw[:], kept[:], over_experts(inv_total[:]), ALU.mult).then_inc(route_step, 1)

            def degrees(n):
                dve.wait_ge(agg_done, n + 1)
                nc.vector.tensor_scalar(deg_max[:], ps_gnn[:, :, P], 1.0, None, ALU.max).then_inc(deg_step, 1)
                nc.vector.tensor_scalar(deg_pos[:], ps_gnn[:, :, P], 0.0, None, ALU.is_gt).then_inc(deg_step, 1)

            def invert_degrees(n):
                dve.wait_ge(deg_step, DEG * n + 1)
                nc.vector.reciprocal(deg_inv[:], deg_max[:]).then_inc(deg_step, 1)

            def message_scale(n):
                dve.wait_ge(deg_step, DEG * n + 3)
                nc.vector.tensor_tensor(deg_scale[:], deg_inv[:], deg_pos[:], ALU.mult).then_inc(deg_step, 1)

            def mean_messages(n):
                dve.wait_ge(deg_step, DEG * n + 4)
                dve.wait_ge(upd_bias_ready, n + 1)
                for g in range(G):
                    last = nc.vector.scalar_tensor_tensor(pre_relu[:, g], ps_gnn[:, g, 0:P], deg_scale[:, g:g + 1],
                                                          upd_bias[:, g], ALU.mult, ALU.add)
                last.then_inc(pre_relu_ready, 1)

            def graph_output(n, j):
                dve.wait_ge(pre_relu_ready, n + 1)
                wait(dve, result_ready, n - SLOTS + 1)
                nc.vector.scalar_tensor_tensor(x2[:, j], pre_relu[:], 0.0, xs[:, j], ALU.max, ALU.add)\
                  .then_inc(x2_ready, 1)

            def weigh(n, j, e):
                if e % (E // 2) == 0:
                    dve.wait_ge(cw_in[j % 2][e // (E // 2)],
                                16 * (n // 2 + 1) if isinstance(n, int) else 8 * (n - j % 2) + 16)
                if e == 0:
                    wait(dve, result_t_done, n - 1)
                    to = acc[:, j % 2]
                else:
                    wait(dve, added, (E - 1) * n + e - (4 if e > 4 else 7 if e == 4 else 3))
                    to = weighted[:, e % 4]
                dve.wait_ge(y_done, E * n + e + 1)
                nc.vector.scalar_tensor_tensor(to.rearrange("p (g t) -> p g t", g=G),
                                               ps_y[:, e % 2].rearrange("p (g t) -> p g t", g=G),
                                               b2_cols[:, e:e + 1], cw_rows[:, j % 2, :, e],
                                               ALU.add, ALU.mult).then_inc(y_used, 1)

            def split_hidden(i, s):
                if first_half(i, s):
                    n, e = first_half(i, s)
                    dve.wait_ge(gel_hi_ready, E * n + e + 1)
                    nc.vector.tensor_tensor(gel_lo[:, e % 4], gel[:, e % 2], gel_hi[:, e % 4].bitcast(F32),
                                            ALU.subtract).then_inc(gel_ready, 1)

            def finish(n, j):
                dve.wait_ge(result_t_done, n + 1)
                wait(dve, out_stored[j % 2], 16 * (n // 2) if isinstance(n, int) else 8 * (n - j % 2))
                nc.vector.tensor_tensor(result[:, j % 2], ps_t[:], x2[:, j], ALU.add).then_inc(result_ready, 1)

            def tile(i, j):
                j2, q = (j + 2) % SLOTS, (j - 1) % SLOTS
                runs, route, graph, norm = inside(i), inside(i + 1), inside(i + 2), inside(i + 4)
                last = inside(i - 1)
                x_count = 16 * ((i + 4) // SLOTS + 1) if isinstance(i, int) else 4 * (i + 4 - j) + 16

                if graph:
                    degrees(i + 2)
                    invert_degrees(i + 2)
                    message_scale(i + 2)
                    mean_messages(i + 2)
                if last:
                    weigh(i - 1, q, 5)
                split_hidden(i, 0)
                if route:
                    biased_logits(i + 1)
                if finished(i):
                    finish(i - 2, j2)
                if route:
                    whole_logits(i + 1)
                if graph:
                    graph_output(i + 2, j2)
                if route:
                    maximum(i + 1)
                if last:
                    weigh(i - 1, q, 6)
                if route:
                    below_maximum(i + 1)
                split_hidden(i, 1)
                if route:
                    first_keys(i + 1)
                if graph:
                    dve.wait_ge(x2_ready, i + 3)
                    row_statistics(x2[:, j2], stats2_step, stats2)
                if route:
                    highest_key(i + 1, 0)
                if last:
                    weigh(i - 1, q, 7)
                if last and not runs:
                    finish(i - 1, q)
                if route:
                    mark(i + 1, 0)
                if graph:
                    wait(dve, rstd2_ready, i + 2)
                    means(i + 2, stats2_step, stats2, neg_mean2)
                split_hidden(i, 2)
                if route:
                    leave_first(i + 1)
                if graph:
                    squares(i + 2, stats2_step)
                if route:
                    best_of_rest(i + 1)
                if graph:
                    variances(i + 2, stats2_step, var2)
                if runs:
                    weigh(i, j, 0)
                if route:
                    below_best_of_rest(i + 1)
                split_hidden(i, 3)
                if inside(i + 3) and not runs:
                    lower_first_norm(i + 3)
                if route:
                    second_keys(i + 1)
                if route:
                    highest_key(i + 1, 1)
                if route:
                    mark(i + 1, 1)
                if runs:
                    weigh(i, j, 1)
                if route:
                    both_choices(i + 1)
                split_hidden(i, 4)
                if inside(i + 3) and runs:
                    lower_first_norm(i + 3)
                if graph:
                    dve.wait_ge(rstd2_ready, i + 3)
                    wait(dve, xn2_t_done, i + 2)
                    normalise(x2[:, j2], neg_mean2, rstd2, xn2).then_inc(xn2_ready, 1)
                if route:
                    totals(i + 1)
                    keep_chosen(i + 1)
                    invert_totals(i + 1)
                if runs:
                    weigh(i, j, 2)
                if route:
                    combine_weights(i + 1)
                split_hidden(i, 5)
                if norm:
                    dve.wait_ge(x_in[j], x_count)
                    row_statistics(xs[:, j], stats1_step, stats1)
                if runs:
                    weigh(i, j, 3)
                if norm:
                    wait(dve, shift1_ready, i + 4)
                    means(i + 4, stats1_step, stats1, neg_mean1)
                split_hidden(i, 6)
                if norm:
                    squares(i + 4, stats1_step)
                if graph:
                    dve.wait_ge(xt_hi_ready, i + 3)
                    nc.vector.tensor_tensor(xt_lo[:, j2], ps_t[:].rearrange("p g t -> p (g t)"),
                                            xt_hi[:, j2].bitcast(F32), ALU.subtract).then_inc(xt_ready, 1)
                if runs:
                    weigh(i, j, 4)
                if norm:
                    variances(i + 4, stats1_step, var1)
                split_hidden(i, 7)
                if isinstance(i, int) and i == -4:
                    lower_graph_weights()
                if isinstance(i, int) and i == -3:
                    lower_weights()

            every_tile(dve, tile)

        @block.tensor
        def _(pe):
            pe.wait_ge(gnn_in, 3 * 16)
            pe.wait_ge(consts_ready, 1)

            def first_product(n, j, e):
                ex = E * n + e
                for c in range(HC):
                    wait(pe, gel_done, HC * (ex - 1) + c + 1)
                    cols = slice(c * P, c * P + P)
                    nc.tensor.matmul(ps_hid[:, c], w1_hi[:, e, cols], xt_hi[:, j], start=True, stop=False)
                    nc.tensor.matmul(ps_hid[:, c], w1_hi[:, e, cols], xt_lo[:, j], start=False, stop=False)
                    nc.tensor.matmul(ps_hid[:, c], w1_lo[:, e, cols], xt_hi[:, j], start=False, stop=True)\
                      .then_inc(hid_done, 1)

            def second_product(n, e):
                ex = E * n + e
                pe.wait_ge(gel_ready, ex + 1)
                wait(pe, y_used, ex - 1)
                for c in range(HC):
                    w = HC * e + c
                    nc.tensor.matmul(ps_y[:, e % 2], w2_hi[:, w], gel_hi[:, e % 4, c], start=c == 0, stop=False)
                    nc.tensor.matmul(ps_y[:, e % 2], w2_hi[:, w], gel_lo[:, e % 4, c], start=False, stop=False)
                    last = nc.tensor.matmul(ps_y[:, e % 2], w2_lo[:, w], gel_hi[:, e % 4, c],
                                            start=False, stop=c == HC - 1)
                last.then_inc(y_done, 1)

            def turn_back(n, k):
                pe.wait_ge(added, (E - 1) * (n + 1))
                pe.wait_ge(xt_ready, at_most(n + 4, TILES))
                wait(pe, result_ready, n)
                for g in range(G):
                    last = nc.tensor.transpose(ps_t[:, g], acc[:, k, g * P:g * P + P], ident[:])
                last.then_inc(result_t_done, 1)

            def tile(i, j):
                j2, j3 = (j + 2) % SLOTS, (j + 3) % SLOTS
                for s in range(E):
                    if s == 7 and inside(i + 1):
                        n = i + 1
                        pe.wait_ge(route_step, ROUTE * (n + 1))
                        nc.tensor.transpose(ps_s[0:G * E, 0:P], cw[:].rearrange("p g e -> p (g e)"), ident[:])\
                          .then_inc(cw_t_done, 1)
                    if isinstance(i, int) and i == -1 and s == E - LAG:
                        pe.wait_ge(w_ready, 3)
                        pe.wait_ge(w2_lo_ready, 1)
                    if first_half(i, s):
                        n, e = first_half(i, s)
                        first_product(n, 0 if isinstance(n, int) and n == 0 else j, e)
                    if s == 0 and inside(i + 1):
                        n, k = i + 1, (j + 1) % SLOTS
                        pe.wait_ge(xt_ready, n + 1)
                        pe.wait_ge(w_ready, 2)
                        wait(pe, cw_t_ready, n)
                        for g in range(G):
                            at = slice(g * P, g * P + P)
                            both_halves = ps_s[:, g * 2 * E:(g + 1) * 2 * E]
                            nc.tensor.matmul(both_halves, xt_hi[:, k, at], gate_split[:].rearrange("p h e -> p (h e)"),
                                             start=True, stop=False)
                            last = nc.tensor.matmul(both_halves[:, 0:E], xt_lo[:, k, at], gate_split[:, 0],
                                                    start=False, stop=True)
                        last.then_inc(gate_done, 1)
                    if s == 0 and finished(i):
                        turn_back(i - 2, j % 2)
                    if s == 4 and inside(i + 3):
                        n = i + 3
                        wait(pe, pre_relu_ready, n)
                        for g in range(G):
                            pe.wait_ge(xn1_ready, G * n + g + 1)
                            last = nc.tensor.transpose(xn1_ps[:, g], xn1[:, g], ident[:])
                        last.then_inc(xn1_t_done, 1)
                    if s == 6 and inside(i + 3):
                        n = i + 3
                        pe.wait_ge(xn1_t_ready, n + 1)
                        pe.wait_ge(w_ready, 1)
                        for g in range(G):
                            nc.tensor.matmul(ps_gnn[:, g], xn1_hi[:, g], w_gnn_hi[:], start=True, stop=False)
                            nc.tensor.matmul(ps_gnn[:, g], xn1_lo[:, g], w_gnn_hi[:], start=False, stop=False)
                            last = nc.tensor.matmul(ps_gnn[:, g], xn1_hi[:, g], w_gnn_lo[:], start=False, stop=True)
                        last.then_inc(gnn_done, 1)
                    if s == 6 and inside(i + 2):
                        n = i + 2
                        pe.wait_ge(xn2_ready, n + 1)
                        wait(pe, result_ready, i - 1)
                        for g in range(G):
                            last = nc.tensor.transpose(ps_t[:, g], xn2[:, g], ident[:])
                        last.then_inc(xn2_t_done, 1)
                    if s == 7 and inside(i + 3):
                        n = i + 3
                        pe.wait_ge(adj_in[j3], 16 * (n // SLOTS + 1) if isinstance(n, int) else 4 * (n - j3) + 16)
                        pe.wait_ge(upd_ready, n + 1)
                        for g in range(G):
                            last = nc.tensor.matmul(ps_gnn[:, g, 0:P + 1], adjs[:, j3, g], msg_rows[:, g],
                                                    start=True, stop=True)
                        last.then_inc(agg_done, 1)
                    e = (s - LAG) % E
                    n = i if s >= LAG else i - 1
                    if inside(n):
                        second_product(n, e)
                if len(finished(i)) > 1:
                    turn_back(i - 1, (j - 1) % 2)

            every_tile(pe, tile)


_INS = ["x", "adj", "L0_gnn_W_msg", "L0_gnn_W_upd", "L0_gnn_bias", "L0_ffn_gate_w", "L0_ffn_gate_b",
        "L0_ffn_W1", "L0_ffn_b1", "L0_ffn_W2", "L0_ffn_b2"]


def kernel(**inputs):
    import numpy as np
    import concourse.bacc as bacc
    from concourse.bass_utils import run_bass_kernel_spmd as run

    nc = bacc.Bacc("TRN2", target_bir_lowering=False, num_devices=1)
    arrays, args = {}, []
    for name in _INS:
        a = np.ascontiguousarray(inputs[name])
        arrays[f"in_{name}"] = a
        args.append(nc.dram_tensor(f"in_{name}", a.shape, mybir.dt.from_np(a.dtype), kind="ExternalInput").ap())
    out = nc.dram_tensor("out", (GRAPHS, P, P), F32, kind="ExternalOutput").ap()
    cw_dram = nc.dram_tensor("cw_dram", (TILES, G * E, P), F32, kind="Internal").ap()
    gnn_moe(nc, *args, out, cw_dram)
    return run(nc, [arrays], core_ids=[0]).results[0]["out"]
```
